# Optimizing a Trainium2 kernel written in Bass

```python
import numpy as np
import jax
import jax.numpy as jnp

def _softmax(x, axis=-1):
    return jax.nn.softmax(x, axis=axis)

def _gelu(x):
    return jax.nn.gelu(x, approximate=True)

def _silu(x):
    return jax.nn.silu(x)

def _sigmoid(x):
    return jax.nn.sigmoid(x)

def _layernorm(x, axis=-1, eps=1e-05):
    m = jnp.mean(x, axis=axis, keepdims=True)
    v = jnp.var(x, axis=axis, keepdims=True)
    return (x - m) / jnp.sqrt(v + eps)

def _scatter_add(tgt, idx, src, axis=0):
    return tgt.at[idx].add(src)

def _segment_sum(src, seg, n):
    return jax.ops.segment_sum(src, seg, n)
kernel_name = 'mk_vit_tower_cls_d1_tok_img256_r4_dd69ae'

def setup_inputs(seed: int=0):
    np.random.seed(seed)
    _w = jnp.asarray

    def _rec_inputs():
        import jax
        import jax.numpy as jnp
        _rk = jax.random.key(seed)
        x = -0.00040386 + 0.999972 * jax.random.normal(jax.random.fold_in(_rk, 1), (16, 3, 64, 64), jnp.float32)
        cls_tok = 0.02 * jax.random.normal(jax.random.fold_in(_rk, 5), (1, 1, 64), jnp.float32)
        return (x, cls_tok)
    x, cls_tok = _rec_inputs()

    def _L0_tok_setup():
        import jax, jax.numpy as jnp
        import numpy as np
        EPS = 1e-05
        P = 8
        DIM = 64
        NUM_TOKENS = 64
        PATCH_DIM = 3 * P * P

        def layernorm(x, g, b):
            mu = jnp.mean(x, axis=-1, keepdims=True)
            var = jnp.mean(jnp.square(x - mu), axis=-1, keepdims=True)
            return (x - mu) * jax.lax.rsqrt(var + EPS) * g + b
        key = jax.random.key(seed)
        ks = jax.random.split(key, 8)
        b, c, h, w = (16, 3, 128, 128)
        x = jax.random.normal(ks[0], (b, c, h, w), dtype=jnp.float32)
        ln1_g = jnp.ones((PATCH_DIM,), jnp.float32)
        ln1_b = jnp.zeros((PATCH_DIM,), jnp.float32)
        W1 = jax.random.normal(ks[1], (PATCH_DIM, DIM), jnp.float32) * 0.02
        b1 = jnp.zeros((DIM,), jnp.float32)
        ln2_g = jnp.ones((DIM,), jnp.float32)
        ln2_b = jnp.zeros((DIM,), jnp.float32)
        Wp1 = jax.random.normal(ks[2], (DIM, DIM), jnp.float32) * 0.02
        bp1 = jnp.zeros((DIM,), jnp.float32)
        lnp_g = jnp.ones((DIM,), jnp.float32)
        lnp_b = jnp.zeros((DIM,), jnp.float32)
        Wp2 = jax.random.normal(ks[3], (DIM, NUM_TOKENS), jnp.float32) * 0.02
        bp2 = jnp.zeros((NUM_TOKENS,), jnp.float32)
        return {'x': x, 'ln1_g': ln1_g, 'ln1_b': ln1_b, 'W1': W1, 'b1': b1, 'ln2_g': ln2_g, 'ln2_b': ln2_b, 'Wp1': Wp1, 'bp1': bp1, 'lnp_g': lnp_g, 'lnp_b': lnp_b, 'Wp2': Wp2, 'bp2': bp2}
    _L0_tok_all = _L0_tok_setup()
    _L0_tok_in = {k: v for k, v in _L0_tok_all.items() if k in ('ln1_g', 'ln1_b', 'W1', 'b1', 'ln2_g', 'ln2_b', 'Wp1', 'bp1', 'lnp_g', 'lnp_b', 'Wp2', 'bp2')}
    del _L0_tok_all

    def _L0_attn_setup():
        import jax, jax.numpy as jnp
        import numpy as np
        B, S, E, H = (8, 512, 64, 8)
        LN_EPS = 1e-05
        key = jax.random.key(seed)
        ks = jax.random.split(key, 5)
        x = jax.random.normal(ks[0], (B, S, E), dtype=jnp.float32)
        Wq = jax.random.normal(ks[1], (E, E), dtype=jnp.float32) * 0.02
        Wk = jax.random.normal(ks[2], (E, E), dtype=jnp.float32) * 0.02
        Wv = jax.random.normal(ks[3], (E, E), dtype=jnp.float32) * 0.02
        bias_table = jax.random.normal(ks[4], (2 * S - 1, H), dtype=jnp.float32) * 0.02
        ln_gamma = jnp.ones((E,), dtype=jnp.float32)
        ln_beta = jnp.zeros((E,), dtype=jnp.float32)
        return {'x': x, 'Wq': Wq, 'Wk': Wk, 'Wv': Wv, 'bias_table': bias_table, 'ln_gamma': ln_gamma, 'ln_beta': ln_beta}
    _L0_attn_all = _L0_attn_setup()
    _L0_attn_in = {k: v for k, v in _L0_attn_all.items() if k in ('Wq', 'Wk', 'Wv', 'bias_table', 'ln_gamma', 'ln_beta')}
    del _L0_attn_all

    def _L0_ffn_setup():
        import jax, jax.numpy as jnp
        import numpy as np
        B, S, D = (8, 1024, 64)
        H = 4 * D
        CAPACITY = 0.5
        key = jax.random.key(seed)
        ks = jax.random.split(key, 6)
        x = jax.random.normal(ks[0], (B, S, D), dtype=jnp.float32)
        attention_mask = jnp.zeros((B, 1, 1, S), dtype=jnp.float32)
        wr = jax.random.normal(ks[1], (D, 1), dtype=jnp.float32) * 0.02
        br = jnp.zeros((1,), dtype=jnp.float32)
        w1 = jax.random.normal(ks[2], (D, H), dtype=jnp.float32) * 0.02
        b1 = jnp.zeros((H,), dtype=jnp.float32)
        w2 = jax.random.normal(ks[3], (H, D), dtype=jnp.float32) * 0.02
        b2 = jnp.zeros((D,), dtype=jnp.float32)
        return {'x': x, 'attention_mask': attention_mask, 'wr': wr, 'br': br, 'w1': w1, 'b1': b1, 'w2': w2, 'b2': b2}
    _L0_ffn_all = _L0_ffn_setup()
    _L0_ffn_in = {k: v for k, v in _L0_ffn_all.items() if k in ('attention_mask', 'wr', 'br', 'w1', 'b1', 'w2', 'b2')}
    del _L0_ffn_all
    return {'x': x, 'cls_tok': cls_tok, 'L0_tok_ln1_g': _L0_tok_in['ln1_g'], 'L0_tok_ln1_b': _L0_tok_in['ln1_b'], 'L0_tok_W1': _L0_tok_in['W1'], 'L0_tok_b1': _L0_tok_in['b1'], 'L0_tok_ln2_g': _L0_tok_in['ln2_g'], 'L0_tok_ln2_b': _L0_tok_in['ln2_b'], 'L0_tok_Wp1': _L0_tok_in['Wp1'], 'L0_tok_bp1': _L0_tok_in['bp1'], 'L0_tok_lnp_g': _L0_tok_in['lnp_g'], 'L0_tok_lnp_b': _L0_tok_in['lnp_b'], 'L0_tok_Wp2': _L0_tok_in['Wp2'], 'L0_tok_bp2': _L0_tok_in['bp2'], 'L0_attn_Wq': _L0_attn_in['Wq'], 'L0_attn_Wk': _L0_attn_in['Wk'], 'L0_attn_Wv': _L0_attn_in['Wv'], 'L0_attn_bias_table': _L0_attn_in['bias_table'], 'L0_attn_ln_gamma': _L0_attn_in['ln_gamma'], 'L0_attn_ln_beta': _L0_attn_in['ln_beta'], 'L0_ffn_attention_mask': _L0_ffn_in['attention_mask'], 'L0_ffn_wr': _L0_ffn_in['wr'], 'L0_ffn_br': _L0_ffn_in['br'], 'L0_ffn_w1': _L0_ffn_in['w1'], 'L0_ffn_b1': _L0_ffn_in['b1'], 'L0_ffn_w2': _L0_ffn_in['w2'], 'L0_ffn_b2': _L0_ffn_in['b2']}

def reference(x, cls_tok, L0_tok_ln1_g, L0_tok_ln1_b, L0_tok_W1, L0_tok_b1, L0_tok_ln2_g, L0_tok_ln2_b, L0_tok_Wp1, L0_tok_bp1, L0_tok_lnp_g, L0_tok_lnp_b, L0_tok_Wp2, L0_tok_bp2, L0_attn_Wq, L0_attn_Wk, L0_attn_Wv, L0_attn_bias_table, L0_attn_ln_gamma, L0_attn_ln_beta, L0_ffn_attention_mask, L0_ffn_wr, L0_ffn_br, L0_ffn_w1, L0_ffn_b1, L0_ffn_w2, L0_ffn_b2):
    import jax
    import jax.numpy as jnp

    def _L0_tok_ref(x, ln1_g, ln1_b, W1, b1, ln2_g, ln2_b, Wp1, bp1, lnp_g, lnp_b, Wp2, bp2):
        import jax, jax.numpy as jnp
        import numpy as np
        EPS = 1e-05
        P = 8
        DIM = 64
        NUM_TOKENS = 64
        PATCH_DIM = 3 * P * P

        def layernorm(x, g, b):
            mu = jnp.mean(x, axis=-1, keepdims=True)
            var = jnp.mean(jnp.square(x - mu), axis=-1, keepdims=True)
            return (x - mu) * jax.lax.rsqrt(var + EPS) * g + b
        b, c, H, W = x.shape
        hp, wp = (H // P, W // P)
        patches = x.reshape(b, c, hp, P, wp, P)
        patches = jnp.transpose(patches, (0, 2, 4, 3, 5, 1))
        patches = patches.reshape(b, hp * wp, P * P * c)
        tokens = layernorm(patches, ln1_g, ln1_b)
        tokens = tokens @ W1 + b1
        tokens = layernorm(tokens, ln2_g, ln2_b)
        q = tokens
        k = tokens
        tokens = jnp.concatenate([q, k, tokens], axis=1)
        h1 = layernorm(tokens @ Wp1 + bp1, lnp_g, lnp_b)
        h1 = jax.nn.silu(h1)
        return h1 @ Wp2 + bp2

    def _L0_attn_ref(x, Wq, Wk, Wv, bias_table, ln_gamma, ln_beta):
        import jax, jax.numpy as jnp
        import numpy as np
        B, S, E, H = (8, 512, 64, 8)
        LN_EPS = 1e-05
        b, s, e = x.shape
        h = bias_table.shape[1]
        d = e // h
        scale = e ** (-0.5)
        q = (x @ Wq.T).reshape(b, s, h, d).transpose(0, 2, 1, 3)
        k = (x @ Wk.T).reshape(b, s, h, d).transpose(0, 2, 1, 3)
        v = (x @ Wv.T).reshape(b, s, h, d).transpose(0, 2, 1, 3)
        attn = jax.nn.softmax(jnp.einsum('bhqd,bhkd->bhqk', q, k) * scale, axis=-1)
        idx = jnp.arange(s)[:, None] - jnp.arange(s)[None, :] + (s - 1)
        rel_bias = bias_table[idx].transpose(2, 0, 1)
        attn = attn + rel_bias[None]
        out = jnp.einsum('bhqk,bhkd->bhqd', attn, v)
        out = out.transpose(0, 2, 1, 3).reshape(b, s, e)
        mu = jnp.mean(out, axis=-1, keepdims=True)
        var = jnp.var(out, axis=-1, keepdims=True)
        out = (out - mu) * jax.lax.rsqrt(var + LN_EPS) * ln_gamma + ln_beta
        return out

    def _L0_ffn_ref(x, attention_mask, wr, br, w1, b1, w2, b2):
        import jax, jax.numpy as jnp
        import numpy as np
        B, S, D = (8, 1024, 64)
        H = 4 * D
        CAPACITY = 0.5
        b, s, d = x.shape
        weights = (jnp.einsum('bsd,do->bso', x, wr) + br)[..., 0]
        k = max(1, int(CAPACITY * s))
        kk = k - 1 if k > 1 else 1
        _, idx = jax.lax.top_k(weights, k)
        sel_idx = idx[:, :kk]
        sel = jnp.take_along_axis(x, sel_idx[:, :, None], axis=1)
        h = jax.nn.gelu(jnp.einsum('bkd,dh->bkh', sel, w1) + b1)
        y = jnp.einsum('bkh,hd->bkd', h, w2) + b2
        w_sel = jnp.take_along_axis(weights, sel_idx, axis=1)
        y = y * w_sel[..., None]
        batch_idx = jnp.arange(b)[:, None]
        processed = jnp.zeros_like(x).at[batch_idx, sel_idx].set(y)
        return processed + x
    h = _L0_tok_ref(x, L0_tok_ln1_g, L0_tok_ln1_b, L0_tok_W1, L0_tok_b1, L0_tok_ln2_g, L0_tok_ln2_b, L0_tok_Wp1, L0_tok_bp1, L0_tok_lnp_g, L0_tok_lnp_b, L0_tok_Wp2, L0_tok_bp2)
    h = jnp.concatenate([jnp.broadcast_to(cls_tok, (h.shape[0], 1, h.shape[2])), h], axis=1)
    h = h + _L0_attn_ref(_layernorm(h, axis=-1), L0_attn_Wq, L0_attn_Wk, L0_attn_Wv, L0_attn_bias_table, L0_attn_ln_gamma, L0_attn_ln_beta)
    h = h + _L0_ffn_ref(_layernorm(h, axis=-1), L0_ffn_attention_mask, L0_ffn_wr, L0_ffn_br, L0_ffn_w1, L0_ffn_b1, L0_ffn_w2, L0_ffn_b2)
    return h

_drawn_inputs = setup_inputs


def setup_inputs(seed=0):
    import zlib

    import numpy as np

    out = dict(_drawn_inputs(seed))
    spreads = {'L0_tok_ln1_g': (1.0, 0.2),
     'L0_tok_ln1_b': (0.0, 0.1),
     'L0_tok_b1': (0.0, 0.1),
     'L0_tok_ln2_g': (1.0, 0.2),
     'L0_tok_ln2_b': (0.0, 0.1),
     'L0_tok_bp1': (0.0, 0.1),
     'L0_tok_lnp_g': (1.0, 0.2),
     'L0_tok_lnp_b': (0.0, 0.1),
     'L0_tok_bp2': (0.0, 0.1),
     'L0_attn_ln_gamma': (1.0, 0.2),
     'L0_attn_ln_beta': (0.0, 0.1),
     'L0_ffn_b1': (0.0, 0.8),
     'L0_ffn_b2': (0.0, 0.8)}
    factors = {'L0_attn_Wq': 8.0, 'L0_attn_Wk': 8.0, 'L0_ffn_wr': 8.0, 'L0_ffn_w1': 8.0, 'L0_ffn_w2': 8.0}
    for name, (base, spread) in spreads.items():
        noise = np.random.default_rng([zlib.crc32(name.encode()), seed]).standard_normal(out[name].shape)
        drawn = base * np.exp(spread * noise) if base else spread * noise
        out[name] = jnp.asarray(drawn.astype(out[name].dtype))
    for name, factor in factors.items():
        out[name] = (out[name] * factor).astype(out[name].dtype)
    return out
```

```python
from contextlib import ExitStack

import numpy as np
import concourse.bass as bass
from concourse import mybir

F32 = mybir.dt.float32
I32 = mybir.dt.int32
ALU = mybir.AluOpType
ACT = mybir.ActivationFunctionType
AX = mybir.AxisListType.X

B, J, E, H, D = 16, 64, 64, 8, 8
NP = B // 2
S = 3 * J + 1
PF = 192
PK = PF // 2
NT = 8
HID = 256
U = S + 2 * J
KEEP = int(0.5 * S) - 1
ROUNDS = (KEEP + 7) // 8
G = 4
GC = 2 * S
CH = [(0, 97), (97, 96), (193, 96), (289, 97)]
VB = (6, 0)
YB = (5, 3, 2, 7)
MB = (6, 0, 1, 4)
CW = 97
EPS = 1e-5

CONST = [("ident", 128), ("cent", 128), ("same_head", 128), ("headmask", 8), ("half", 2)]
TOKW = [("wp1", 64), ("wp2", 64), ("g2", 1), ("b2", 1), ("g3", 1), ("b3", 1), ("bp2", 1),
        ("a_gamma", 1), ("a_beta", 1), ("ffn_b2", 1), ("wp2_bd", 128)]
ATTW = [("wq_bd", 128), ("wk_bd", 128), ("wv_bd", 128), ("wv", 64)]
FFNW = [("ffn_w1", 256), ("ffn_w2", 128), ("ffn_b1", 2), ("wr_bd", 2)]


def columns(fields):
    at, out = 0, {}
    for name, n in fields:
        out[name] = (at, at + n)
        at += n
    return out, at


def bc(ap, axis, n):
    shape = list(ap.shape)
    return ap.unsqueeze(axis).broadcast_to(shape[:axis] + [n] + shape[axis:])


def build(nc, patches_tm, patches_fm, w1_pack, const, rows, tokw, attw, ffnw, toeplitz, table_cls,
          pick, br, out):
    with ExitStack() as ctx:
        def sb(name, *shape):
            return ctx.enter_context(nc.sbuf_tensor(name, list(shape), F32))

        def sem(name):
            return ctx.enter_context(nc.semaphore(name))

        bank = [ctx.enter_context(nc.psum_tensor(f"bank{i}", [128, 512], F32)) for i in range(8)]

        ptm = sb("ptm", 128, NT, PF)
        pfm = sb("pfm", PK, 2, NT * 128)
        w1p = sb("w1p", PK, 2 * E + 4)
        cst = sb("cst", 128, columns(CONST)[1])
        row = sb("row", 128, 5 * E)
        tkw = sb("tkw", 128, columns(TOKW)[1])
        atw = sb("atw", 128, columns(ATTW)[1])
        ffw = sb("ffw", 128, columns(FFNW)[1])
        toep = sb("toep", 128, 4, U)
        tcls = sb("tcls", 128, 2, H)
        sel16 = sb("sel16", B, NP, 128)
        br16 = sb("br16", B, 1)

        def view(tile, fields, name):
            a, b = columns(fields)[0][name]
            return tile[:, a:b]

        ident, cent = view(cst, CONST, "ident"), view(cst, CONST, "cent")
        half = view(cst, CONST, "half")
        w1 = w1p[:, 0:2 * E].rearrange("p (c f) -> p c f", c=2)

        eps = sb("eps", 128, 1)
        inv_pf = sb("inv_pf", PK, PK)
        ones_row = sb("ones_row", 1, 128)
        gw = sb("gw", PK, 2, E)
        gwc = sb("gwc", PK, 2, E)
        gws = sb("gws", PK, 2)
        gwf = sb("gwf", PK, 2, E)
        cr = sb("cr", 128, 4, E)
        crs = sb("crs", 128, 4)
        crc = sb("crc", 128, 4, E)
        wg = sb("wg", 128, E)
        wgs = sb("wgs", 128, 1)
        wg_bd = sb("wg_bd", 128, 128)
        wp2s = sb("wp2s", 128, 1)
        wp2c_bd = sb("wp2c_bd", 128, 128)
        st = sb("st", 128, NT, 6)
        st_d = sb("st_d", 128, NT)
        st_s = sb("st_s", 128, NT)
        st_q = sb("st_q", 128, NT)
        st_v = sb("st_v", 128, NT)
        root = sb("root", 128, 6, NT)
        rs = sb("rs", 128, 6, NT)
        ys = sb("ys", 128, NT, E)
        y = sb("y", 128, NT, E)
        sq = sb("sq", 128, NT, E)
        ss = sb("ss", 128, 4, NT)
        yT = sb("yT", 128, 4, 128)
        zs = sb("zs", 128, NT, E)
        z = sb("z", 128, NT, E)
        zn = sb("zn", 128, NT, E)
        h1T = sb("h1T", 128, 512)
        hbias = sb("hbias", 128, 1)
        hb = sb("hb", 128, NP, J + 1)
        xn = sb("xn", 128, NT, E)
        xT = sb("xT", 128, NP, J)
        csq = sb("csq", 128, E)
        xcls = sb("xcls", 128, 2, E)
        xclsT = sb("xclsT", 128, 1)
        qcls = sb("qcls", 128, 1)
        kcls = sb("kcls", 128, 1)
        nvclsT = sb("nvclsT", 128, 1)
        vcls = sb("vcls", 128, E)
        qcls_m = sb("qcls_m", 128, 128)
        kcls_m = sb("kcls_m", 128, H)
        kT = sb("kT", 128, NP * J)
        q_bd = sb("q_bd", 128, NP, 128)
        k_h = sb("k_h", 128, H, NP * J)
        vT = sb("vT", 128, NP, J)
        vx = sb("vx", 128, NP, 4, 4, 9)
        s_cls = sb("s_cls", 128, NP, H)
        mx0 = sb("mx0", 128, NP, H)
        mx = sb("mx", 128, NP, H)
        e_in = sb("e_in", 128, 2, H, J)
        e = sb("e", 128, 2, H * J)
        eT = sb("eT", 128, 2, 4, 128)
        ec_in = sb("ec_in", 128, NP, H)
        ec = sb("ec", 128, NP, H)
        den = sb("den", 128, NP, H)
        rden = sb("rden", 128, NP, H)
        o = sb("o", 128, NP, 4, 2, D)
        pvT = sb("pvT", 128, NP, J)
        cq_cc = sb("cq_cc", 128, 1)
        cq_m0 = sb("cq_m0", 128, NP)
        cq_m = sb("cq_m", 128, NP)
        cq_in = sb("cq_in", 128, NP, J)
        cq_e = sb("cq_e", 128, NP, J)
        cq_ci = sb("cq_ci", 128, NP)
        cq_c = sb("cq_c", 128, NP)
        cq_s = sb("cq_s", 128, NP)
        cq_den = sb("cq_den", 128, NP)
        cq_r = sb("cq_r", 128, NP)
        cq_v = sb("cq_v", 128, NP, J)
        cq_n = sb("cq_n", 128, NP)
        cq_o = sb("cq_o", 128, NP)
        fold1 = sb("fold1", 128, 4, S)
        fold = sb("fold", 128, 4, S)
        rT = sb("rT", 128, 4, S)
        cfac0 = sb("cfac0", 128, 2, H)
        cfac = sb("cfac", 128, 2, H)
        cterm = sb("cterm", 128, 2, H, D)
        tb = sb("tb", 128, 2, B, E)
        zz = sb("zz", 128, G, 2, S)
        zq = sb("zq", 128, G, GC)
        zg = sb("zg", 128, G, GC)
        lroot = sb("lroot", 128, 2, G, 4 * 2)
        lr = sb("lr", 128, 2, G, 4 * 2)
        lrT = sb("lrT", 16, 2, 2, CW)
        zr = sb("zr", 128, G, 2, S)
        h2 = sb("h2", 128, G, 2, S)
        hq, hc = zq, zg
        x2 = sb("x2", 128, G, GC)
        xh = sb("xh", 128, G, GC)
        gl = k_h[:, :, :].rearrange("p h n -> p (h n)")[:, 0:4 * GC].rearrange("p (a n) -> p a n", a=4)
        wt = sb("wt", 128, 2, B)
        w16 = sb("w16", B, S)
        cur = sb("cur", B, 2, S)
        top8 = sb("top8", B, ROUNDS, 8)
        gt = sb("gt", B, S)
        ngt = sb("ngt", B, 1)
        eq = sb("eq", B, S)
        cum = sb("cum", B, S)
        zero16 = sb("zero16", B, S)
        left = sb("left", B, 1)
        tie = sb("tie", B, S)
        chosen = sb("chosen", B, S)
        mw = sb("mw", B, S)
        mwb = sb("mwb", 128, G, GC)
        yw = zz[:, :, :, :].rearrange("p g a q -> p g (a q)")
        res = hc

        names = """in_w1 in_tm0 in_tm1 in_fm0 in_fm1 in_const in_rows in_tokw in_attw in_toep in_ffnw in_pick set_pool gw_ready colmean_ready c_raw_ready gwc_ready gwf_ready cr_ready crc_ready wg_ready wg_bd_ready wp2s_ready wp2c_ready st_ready st_d_ready st_v_ready root1 rs1 y_proj ys_ready y_ready sq_y ss_y root2 rs2 yT_psum yT_ready z_psum zs_ready z_ready sq_z ss_z root3 rs3 zn_ready zn_psum h1_ready h_psum hf_psum hb_ready hbias_ready sq_h ss_h root4 rs4 xn_ready x_psum xT_ready csq_ready css_ready root_c rs_c xcls_ready xclsT_psum xclsT_ready hbc_ready cls_psum cls_qkv qm_ready k_psum kT_ready q_psum q_ready vt_psum vT_ready v_psum vx_ready kh_ready cq_psum cq_mx cq_in_ready cq_e_ready cq_s_ready cq_den_ready cq_r_ready cq_v_ready cq_n_ready cq_o_ready cq_cc_ready scls_psum scls_ready s_psum mx0_ready mx_ready ein_ready e_ready eT_psum eT_ready pv_psum ecin_ready ec_ready den_ready rden_ready o_ready pvT_psum pvT_ready fold1_ready rT_ready rsum_psum cfac_ready cterm_ready tb_psum tb0_ready tb_ready bT_psum zz_ready zc_psum zq_ready zg_ready zvar_psum lroot_ready lr_ready lrb_psum lrt_psum zr_ready h2_ready lrT_ready hc_psum hq_ready hc_ready hvar_psum hroot_ready hr_ready hrb_psum x2_ready xh_ready w_psum wt_ready w16_psum w16_ready top_ready rep_ready gt_ready eq_ready cum_ready chosen_ready mw_ready mwb_psum mwb_ready f1_psum gl_ready f2_psum yw_ready res_ready out_done""".split()
        s = {n: sem(n) for n in names}

        block = ctx.enter_context(nc.Block())

        @block.sync
        def _(sp):
            sp.dma_start(ptm[:, 0:4, :], patches_tm[:, 0:4, :]).then_inc(s["in_tm0"], 16)
            sp.dma_start(ptm[:, 4:8, :], patches_tm[:, 4:8, :]).then_inc(s["in_tm1"], 16)
            sp.dma_start(tkw[:, :], tokw).then_inc(s["in_tokw"], 16)
            sp.dma_start(atw[:, :], attw).then_inc(s["in_attw"], 16)
            sp.dma_start(toep[:, :, :], toeplitz).then_inc(s["in_toep"], 16)
            sp.dma_start(tcls[:, :, :], table_cls).then_inc(s["in_toep"], 16)
            sp.dma_start(ffw[:, :], ffnw).then_inc(s["in_ffnw"], 16)
            sp.dma_start(sel16[:, :, :], pick).then_inc(s["in_pick"], 16)
            sp.dma_start(br16[:, :], br.unsqueeze(0).broadcast_to([B, 1])).then_inc(s["in_pick"], 16)
            for g in range(G):
                sp.wait_ge(s["res_ready"], g + 1)
                sp.dma_start(out[:, g, :], res[:, g, :]).then_inc(s["out_done"], 16)
            sp.wait_ge(s["out_done"], 16 * G)

        @block.gpsimd
        def _(pool):
            pool.memset(inv_pf[:, :], 1.0 / PF).then_inc(s["set_pool"], 1)
            pool.memset(eps[:, :], EPS).then_inc(s["set_pool"], 1)
            pool.memset(ones_row[:, :], 1.0).then_inc(s["set_pool"], 1)
            pool.memset(wg_bd[:, :], 0.0).then_inc(s["set_pool"], 1)
            pool.memset(wp2c_bd[:, :], 0.0).then_inc(s["set_pool"], 1)
            pool.memset(q_bd[:, :, :], 0.0).then_inc(s["set_pool"], 1)
            pool.memset(vx[:, :, :, :, :], 0.0).then_inc(s["set_pool"], 1)
            pool.memset(zero16[:, :], 0.0).then_inc(s["set_pool"], 1)
            pool.wait_ge(s["set_pool"], 8)
            for h in range(2):
                pool.memset(vx[64 * h:64 * h + 64, :, :, h::2, 8:9].rearrange("p a b c d -> p (a b) (c d)"),
                            1.0).then_inc(s["set_pool"], 1)
            pool.wait_ge(s["set_pool"], 10)
            pool.wait_ge(s["in_toep"], 32)
            pool.tensor_tensor(fold1[:, :, :], toep[:, :, 0:S], toep[:, :, J:J + S], ALU.add)\
                .then_inc(s["fold1_ready"], 1)
            pool.wait_ge(s["fold1_ready"], 1)
            pool.tensor_tensor(fold[:, :, :], fold1[:, :, :], toep[:, :, 2 * J:2 * J + S], ALU.add)\
                .then_inc(s["fold1_ready"], 1)
            pool.wait_ge(s["fold1_ready"], 2)
            pool.tensor_copy(rT[:, :, 0:S - 1], fold[:, :, 1:S]).then_inc(s["rT_ready"], 1)
            pool.tensor_copy(rT[:, :, S - 1:S], fold[:, :, 0:1]).then_inc(s["rT_ready"], 1)
            pool.wait_ge(s["cfac_ready"], 2)
            pool.wait_ge(s["cls_qkv"], 4)
            for t, n in ((0, 128), (1, J + 1)):
                pool.tensor_tensor(cterm[0:n, t, :, :], vcls[0:n, :].rearrange("p (h d) -> p h d", h=H),
                                   bc(cfac[0:n, t, :], 2, D), ALU.mult).then_inc(s["cterm_ready"], 1)
            pool.wait_ge(s["cterm_ready"], 2)
            for t in range(2):
                rows_t = 128 if t == 0 else J + 1
                for g in range(2):
                    pool.wait_ge(s["tb0_ready"], 2 * t + g + 1)
                    pool.tensor_tensor(
                        tb[0:rows_t, t, 8 * g:8 * g + 8, :], tb[0:rows_t, t, 8 * g:8 * g + 8, :],
                        bc(cterm[0:rows_t, t].rearrange("p h d -> p (h d)"), 1, 8), ALU.add)\
                        .then_inc(s["tb_ready"], 1)
            for g in range(G):
                pool.wait_ge(s["x2_ready"], g + 1)
                pool.tensor_tensor(xh[:, g, :], x2[:, g, :], h2[:, g].rearrange("p a q -> p (a q)"),
                                   ALU.add).then_inc(s["xh_ready"], 1)

        @block.scalar
        def _(act):
            act.dma_start(w1p[:, :], w1_pack).then_inc(s["in_w1"], 16)
            act.dma_start(pfm[:, :, 0:512], patches_fm[:, :, 0:512]).then_inc(s["in_fm0"], 16)
            act.dma_start(row[:, :], rows.unsqueeze(0).broadcast_to([128, 5 * E])).then_inc(s["in_rows"], 16)
            act.dma_start(pfm[:, :, 512:1024], patches_fm[:, :, 512:1024]).then_inc(s["in_fm1"], 16)
            act.dma_start(cst[:, :], const).then_inc(s["in_const"], 16)

            def sqrt(dst, src, scale, parts=128):
                return act.activation(dst, src, ACT.Sqrt, bias=eps[0:parts, :], scale=scale)

            act.wait_ge(s["set_pool"], 3)
            act.wait_ge(s["crc_ready"], 1)
            act.activation(csq[:, :], crc[:, 3, :], ACT.Square).then_inc(s["csq_ready"], 1)
            act.wait_ge(s["st_v_ready"], 1)
            sqrt(root[:, 0, :], st_v[:, :], 1.0 / PF).then_inc(s["root1"], 1)
            for a in range(2):
                act.wait_ge(s["y_ready"], a + 1)
                act.activation(sq[:, 4 * a:4 * a + 4, :], y[:, 4 * a:4 * a + 4, :], ACT.Square)\
                    .then_inc(s["sq_y"], 1)
            act.wait_ge(s["yT_psum"], 1)
            act.activation(yT[:, 0:2, :], bank[4][:, 0:256].rearrange("p (a n) -> p a n", a=2), ACT.Copy)\
                .then_inc(s["yT_ready"], 1)
            act.wait_ge(s["yT_psum"], 2)
            act.activation(yT[:, 2:4, :], bank[5][:, 0:256].rearrange("p (a n) -> p a n", a=2), ACT.Copy)\
                .then_inc(s["yT_ready"], 1)
            act.wait_ge(s["ss_y"], 1)
            sqrt(root[:, 1, :], ss[:, 0, :], 1.0 / E).then_inc(s["root2"], 1)
            act.wait_ge(s["z_ready"], 1)
            act.activation(sq[:, :, :], z[:, :, :], ACT.Square).then_inc(s["sq_z"], 1)
            act.wait_ge(s["css_ready"], 1)
            sqrt(root[:, 4, 0:1], ss[:, 3, 0:1], 1.0 / E).then_inc(s["root_c"], 1)
            act.wait_ge(s["ss_z"], 1)
            sqrt(root[:, 2, :], ss[:, 1, :], 1.0 / E).then_inc(s["root3"], 1)
            act.wait_ge(s["zn_psum"], 1)
            act.activation(h1T[:, :], bank[7][:, :], ACT.Silu, bias=view(tkw, TOKW, "b3"),
                           scale=view(tkw, TOKW, "g3")).then_inc(s["h1_ready"], 1)
            act.wait_ge(s["h_psum"], 1)
            act.activation(sq[:, :, :].rearrange("p a b -> p (a b)"), bank[0][:, :], ACT.Square)\
                .then_inc(s["sq_h"], 1)
            act.wait_ge(s["ss_h"], 1)
            sqrt(root[:, 3, :], ss[:, 2, :], 1.0 / E).then_inc(s["root4"], 1)
            act.wait_ge(s["hf_psum"], 1)
            act.wait_ge(s["hbias_ready"], 1)
            act.activation(hb[:, :, 0:J], bank[1][:, :].rearrange("p (a j) -> p a j", a=NP), ACT.Identity,
                           bias=hbias[:, :]).then_inc(s["hb_ready"], 1)
            act.wait_ge(s["x_psum"], 1)
            act.activation(xT[:, 0:4, :], bank[2][:, 0:256].rearrange("p (a j) -> p a j", a=4), ACT.Copy)\
                .then_inc(s["xT_ready"], 1)
            act.wait_ge(s["k_psum"], 1)
            act.activation(kT[:, :], bank[5][:, :], ACT.Copy).then_inc(s["kT_ready"], 1)
            act.wait_ge(s["q_psum"], 1)
            act.wait_ge(s["set_pool"], 6)
            act.activation(q_bd[0:64, :, 0:64], bank[4][0:64, :].rearrange("p (a j) -> p a j", a=NP),
                           ACT.Copy, scale=E ** -0.5).then_inc(s["q_ready"], 1)
            act.wait_ge(s["kT_ready"], 1)
            for h in (5, 6, 7):
                act.activation(k_h[:, h, :], kT[:, :], ACT.Copy,
                               scale=view(cst, CONST, "headmask")[:, h:h + 1]).then_inc(s["kh_ready"], 1)
            act.wait_ge(s["vt_psum"], 1)
            act.activation(vT[:, :, :], bank[7][:, :].rearrange("p (a j) -> p a j", a=NP), ACT.Identity,
                           bias=nvclsT[:, :]).then_inc(s["vT_ready"], 1)
            act.wait_ge(s["scls_psum"], 1)
            act.activation(s_cls[:, :, :], bank[2][:, 0:64].rearrange("p (a h) -> p a h", a=NP), ACT.Copy)\
                .then_inc(s["scls_ready"], 1)

            def table_out(t, g):
                n = 2 * t + g
                rows_t = 128 if t == 0 else J + 1
                act.wait_ge(s["tb_psum"], n + 1)
                act.activation(tb[0:rows_t, t, 8 * g:8 * g + 8, :],
                               bank[5][0:rows_t, :].rearrange("p (a f) -> p a f", a=8), ACT.Copy)\
                    .then_inc(s["tb0_ready"], 1)

            def weights_out(p):
                act.wait_ge(s["eT_psum"], p + 1)
                if p >= 2:
                    act.wait_ge(s["pv_psum"], p - 1)
                act.activation(eT[:, p % 2].rearrange("p a n -> p (a n)"), bank[6 + p % 2][:, :], ACT.Copy)\
                    .then_inc(s["eT_ready"], 1)

            for p in range(NP + 1):
                if p < NP:
                    act.wait_ge(s["ein_ready"], p + 1)
                    if p >= 2:
                        act.wait_ge(s["eT_psum"], p - 1)
                    act.activation(e[:, p % 2, :], e_in[:, p % 2].rearrange("p h k -> p (h k)"), ACT.Exp)\
                        .then_inc(s["e_ready"], 1)
                if p == 1:
                    act.wait_ge(s["cq_in_ready"], 2)
                    act.activation(cq_e[:, :, :], cq_in[:, :, :], ACT.Exp).then_inc(s["cq_e_ready"], 1)
                    act.activation(cq_c[:, :], cq_ci[:, :], ACT.Exp).then_inc(s["cq_e_ready"], 1)
                if p >= 1:
                    weights_out(p - 1)
                if p in (2, 3, 5, 6):
                    table_out(*((0, 0), (0, 1), (1, 0), (1, 1))[(2, 3, 5, 6).index(p)])
                if p in (4, 7):
                    k = 0 if p == 4 else 1
                    act.wait_ge(s["ecin_ready"], k + 1)
                    act.activation(ec[:, 3 * k:3 * k + 3, :], ec_in[:, 3 * k:3 * k + 3, :], ACT.Exp)\
                        .then_inc(s["ec_ready"], 1)
            act.wait_ge(s["ecin_ready"], 3)
            act.activation(ec[:, 6:8, :], ec_in[:, 6:8, :], ACT.Exp).then_inc(s["ec_ready"], 1)
            act.wait_ge(s["pvT_psum"], 1)
            act.activation(pvT[:, :, :], bank[6][:, :].rearrange("p (a j) -> p a j", a=NP), ACT.Copy)\
                .then_inc(s["pvT_ready"], 1)

            gamma = view(tkw, TOKW, "a_gamma")
            for a in range(2):
                for g in (2 * a, 2 * a + 1):
                    act.wait_ge(s["zc_psum"], g + 1)
                    act.activation(zq[:, g, :], bank[4 + g][:, 0:GC], ACT.Square).then_inc(s["zq_ready"], 1)
                    act.activation(zg[:, g, :], bank[4 + g][:, 0:GC], ACT.Copy, scale=gamma)\
                        .then_inc(s["zg_ready"], 1)
                act.wait_ge(s["zvar_psum"], a + 1)
                sqrt(lroot[0:CW, 0, 2 * a:2 * a + 2, :],
                     bank[2 * a][0:CW, 0:16].rearrange("p (g n) -> p g n", g=2), 1.0 / E, CW)\
                    .then_inc(s["lroot_ready"], 1)
                act.wait_ge(s["lrt_psum"], a + 1)
                act.activation(lrT[:, 0, a, :], bank[2 * a][0:16, 0:CW], ACT.Copy).then_inc(s["lrT_ready"], 1)
            for a in range(2):
                for g in (2 * a, 2 * a + 1):
                    act.wait_ge(s["hc_psum"], g + 1)
                    act.activation(hq[:, g, :], bank[4 + g][:, 0:GC], ACT.Square).then_inc(s["hq_ready"], 1)
                    act.activation(hc[:, g, :], bank[4 + g][:, 0:GC], ACT.Copy).then_inc(s["hc_ready"], 1)
                act.wait_ge(s["hvar_psum"], a + 1)
                sqrt(lroot[0:CW, 1, 2 * a:2 * a + 2, :],
                     bank[2 * a][0:CW, 0:16].rearrange("p (g n) -> p g n", g=2), 1.0 / E, CW)\
                    .then_inc(s["hroot_ready"], 1)
                act.wait_ge(s["lrt_psum"], a + 3)
                act.activation(lrT[:, 1, a, :], bank[2 * a][0:16, 0:CW], ACT.Copy).then_inc(s["lrT_ready"], 1)
            b1 = view(ffw, FFNW, "ffn_b1")

            def router():
                act.wait_ge(s["w_psum"], 1)
                act.activation(wt[:, 0, :], bank[6][:, 0:B], ACT.Copy).then_inc(s["wt_ready"], 1)
                act.activation(wt[0:J + 1, 1, :], bank[6][0:J + 1, B:2 * B], ACT.Copy)\
                    .then_inc(s["wt_ready"], 1)
                act.wait_ge(s["w16_psum"], 1)
                act.wait_ge(s["in_pick"], 32)
                for dst, src in ((w16[:, 1:129], bank[6][0:B, 0:128]), (w16[:, 129:S], bank[6][0:B, 128:S - 1]),
                                 (w16[:, 0:1], bank[6][0:B, S - 1:S])):
                    act.activation(dst, src, ACT.Identity, bias=br16[:, :]).then_inc(s["w16_ready"], 1)

            def mask_out(g):
                act.wait_ge(s["mwb_psum"], g + 1)
                act.activation(mwb[:, g, :], bank[MB[g]][:, 0:GC], ACT.Copy).then_inc(s["mwb_ready"], 1)

            for n in range(4 * G):
                act.wait_ge(s["f1_psum"], n + 1)
                if n >= 4:
                    act.wait_ge(s["f2_psum"], n - 3)
                act.activation(gl[:, n % 4, :], bank[(0, 1, 4)[n % 3]][:, 0:GC], ACT.Gelu_apprx_tanh,
                               bias=b1[:, n % 2:n % 2 + 1]).then_inc(s["gl_ready"], 1)
                if n == 0:
                    router()
            for g in range(G):
                mask_out(g)

        @block.vector
        def _(dve):
            dve.wait_ge(s["in_w1"], 16)
            for c in range(2):
                dve.tensor_scalar(gw[:, c, :], w1[:, c, :], w1p[:, 2 * E + c:2 * E + c + 1], None, ALU.mult)\
                    .then_inc(s["gw_ready"], 1)
            dve.wait_ge(s["colmean_ready"], 1)
            dve.tensor_tensor(gwc[:, :, :], gw[:, :, :], bc(bank[0][0:PK, 0:E], 1, 2), ALU.subtract)\
                .then_inc(s["gwc_ready"], 1)
            dve.wait_ge(s["gwc_ready"], 1)
            dve.tensor_reduce(gws[:, :], gwc[:, :, :], AX, ALU.add).then_inc(s["gwc_ready"], 1)
            dve.wait_ge(s["gwc_ready"], 2)
            dve.scalar_tensor_tensor(gwf[:, :, :], bc(gws[:, :], 2, E), -1.0 / E, gwc[:, :, :],
                                     ALU.mult, ALU.add).then_inc(s["gwf_ready"], 1)
            for t in range(NT):
                dve.wait_ge(s["in_tm0" if t < 4 else "in_tm1"], 16)
                dve.bn_stats(st[:, t, :], ptm[:, t, :]).then_inc(s["st_ready"], 1)
            dve.wait_ge(s["st_ready"], NT)
            dve.tensor_tensor(st_d[:, :], st[:, :, 1], st[:, :, 4], ALU.subtract).then_inc(s["st_d_ready"], 1)
            dve.tensor_tensor(st_s[:, :], st[:, :, 2], st[:, :, 5], ALU.add).then_inc(s["st_d_ready"], 1)
            dve.wait_ge(s["st_d_ready"], 2)
            dve.tensor_tensor(st_q[:, :], st_d[:, :], st_d[:, :], ALU.mult).then_inc(s["st_d_ready"], 1)
            dve.wait_ge(s["st_d_ready"], 3)
            dve.scalar_tensor_tensor(st_v[:, :], st_q[:, :], PF / 4.0, st_s[:, :], ALU.mult, ALU.add)\
                .then_inc(s["st_v_ready"], 1)
            dve.wait_ge(s["in_rows"], 16)
            dve.wait_ge(s["c_raw_ready"], 1)
            dve.tensor_tensor(cr[:, 0:2, :].rearrange("p a f -> p (a f)"), bank[1][:, 0:2 * E], row[:, 0:2 * E],
                              ALU.add).then_inc(s["cr_ready"], 1)
            dve.tensor_copy(cr[:, 2:4, :].rearrange("p a f -> p (a f)"), row[:, 2 * E:4 * E])\
                .then_inc(s["cr_ready"], 1)
            dve.wait_ge(s["cr_ready"], 2)
            dve.tensor_reduce(crs[:, :], cr[:, :, :], AX, ALU.add).then_inc(s["cr_ready"], 1)
            dve.wait_ge(s["cr_ready"], 3)
            dve.scalar_tensor_tensor(crc[:, :, :], bc(crs[:, :], 2, E), -1.0 / E, cr[:, :, :],
                                     ALU.mult, ALU.add).then_inc(s["crc_ready"], 1)

            def recip(i, when, out_sem, n=NT):
                dve.wait_ge(s[when], 1)
                dve.reciprocal(rs[:, i, 0:n], root[:, i, 0:n]).then_inc(s[out_sem], 1)
                dve.wait_ge(s[out_sem], 1)

            recip(0, "root1", "rs1")
            dve.wait_ge(s["crc_ready"], 1)
            for a in range(2):
                t = slice(4 * a, 4 * a + 4)
                dve.wait_ge(s["y_proj"], a + 1)
                dve.tensor_tensor(ys[:, t, :], bank[2 + a][:, 0:256].rearrange("p (t f) -> p t f", t=4),
                                  bc(rs[:, 0, t], 2, E), ALU.mult).then_inc(s["ys_ready"], 1)
                dve.wait_ge(s["ys_ready"], a + 1)
                dve.tensor_tensor(y[:, t, :], ys[:, t, :], bc(crc[:, 0, :], 1, 4), ALU.add)\
                    .then_inc(s["y_ready"], 1)
            dve.wait_ge(s["in_tokw"], 16)
            dve.tensor_scalar(wg[:, :], view(tkw, TOKW, "wp1"), view(tkw, TOKW, "g2"), None, ALU.mult)\
                .then_inc(s["wg_ready"], 1)
            dve.tensor_reduce(wp2s[:, :], view(tkw, TOKW, "wp2"), AX, ALU.add).then_inc(s["wp2s_ready"], 1)
            dve.wait_ge(s["wg_ready"], 1)
            dve.tensor_reduce(wgs[:, :], wg[:, :], AX, ALU.add).then_inc(s["wg_ready"], 1)
            dve.wait_ge(s["wg_ready"], 2)
            dve.wait_ge(s["set_pool"], 5)
            for i in range(2):
                r = slice(64 * i, 64 * i + 64)
                dve.scalar_tensor_tensor(wg_bd[r, r], wgs[r, :].broadcast_to([64, E]), -1.0 / E, wg[r, :],
                                         ALU.mult, ALU.add).then_inc(s["wg_bd_ready"], 1)
            dve.wait_ge(s["sq_y"], 2)
            dve.tensor_reduce(ss[:, 0, :], sq[:, :, :], AX, ALU.add).then_inc(s["ss_y"], 1)
            dve.wait_ge(s["wp2s_ready"], 1)
            for i in range(2):
                r = slice(64 * i, 64 * i + 64)
                dve.scalar_tensor_tensor(wp2c_bd[r, r], wp2s[r, :].broadcast_to([64, E]), -1.0 / E,
                                         view(tkw, TOKW, "wp2")[r, :], ALU.mult, ALU.add)\
                    .then_inc(s["wp2c_ready"], 1)
            recip(1, "root2", "rs2")
            dve.wait_ge(s["z_psum"], 1)
            dve.tensor_tensor(zs[:, :, :], bank[6][:, :].rearrange("p (t f) -> p t f", t=NT),
                              bc(rs[:, 1, :], 2, E), ALU.mult).then_inc(s["zs_ready"], 1)
            dve.wait_ge(s["zs_ready"], 1)
            dve.tensor_tensor(z[:, :, :], zs[:, :, :], bc(crc[:, 1, :], 1, NT), ALU.add)\
                .then_inc(s["z_ready"], 1)
            dve.wait_ge(s["csq_ready"], 1)
            dve.tensor_reduce(ss[:, 3, 0:1], csq[:, :], AX, ALU.add).then_inc(s["css_ready"], 1)
            dve.wait_ge(s["sq_z"], 1)
            dve.tensor_reduce(ss[:, 1, :], sq[:, :, :], AX, ALU.add).then_inc(s["ss_z"], 1)
            recip(4, "root_c", "rs_c", 1)
            dve.tensor_scalar(xcls[:, :, :], bc(crc[:, 3, :], 1, 2), rs[:, 4, 0:1], None, ALU.mult)\
                .then_inc(s["xcls_ready"], 1)
            recip(2, "root3", "rs3")
            dve.wait_ge(s["z_ready"], 1)
            dve.tensor_tensor(zn[:, :, :], z[:, :, :], bc(rs[:, 2, :], 2, E), ALU.mult)\
                .then_inc(s["zn_ready"], 1)
            dve.wait_ge(s["xclsT_psum"], 1)
            dve.tensor_copy(xclsT[:, :], bank[3][:, 0:1]).then_inc(s["xclsT_ready"], 1)
            dve.tensor_scalar(hb[:, :, J], bank[3][:, 1:2].broadcast_to([128, NP]),
                              view(tkw, TOKW, "a_beta"), None, ALU.add).then_inc(s["hbc_ready"], 1)
            dve.tensor_tensor(hbias[:, :], view(tkw, TOKW, "bp2"), view(tkw, TOKW, "a_beta"), ALU.add)\
                .then_inc(s["hbias_ready"], 1)
            dve.wait_ge(s["cls_psum"], 1)
            dve.tensor_scalar(qcls[:, :], bank[2][:, 0:1], E ** -0.5, None, ALU.mult).then_inc(s["cls_qkv"], 1)
            dve.tensor_copy(kcls[:, :], bank[2][:, 1:2]).then_inc(s["cls_qkv"], 1)
            dve.tensor_scalar(nvclsT[:, :], bank[2][:, 2:3], -1.0, None, ALU.mult).then_inc(s["cls_qkv"], 1)
            dve.tensor_copy(vcls[:, :], bank[2][:, 64:128]).then_inc(s["cls_qkv"], 1)
            dve.wait_ge(s["cls_qkv"], 2)
            dve.tensor_scalar(qcls_m[:, :], view(cst, CONST, "same_head"), qcls[:, :], None, ALU.mult)\
                .then_inc(s["qm_ready"], 1)
            dve.tensor_scalar(kcls_m[:, :], view(cst, CONST, "headmask"), kcls[:, :], None, ALU.mult)\
                .then_inc(s["qm_ready"], 1)
            dve.wait_ge(s["sq_h"], 1)
            dve.tensor_reduce(ss[:, 2, :], sq[:, :, :], AX, ALU.add).then_inc(s["ss_h"], 1)
            recip(3, "root4", "rs4")
            dve.tensor_tensor(xn[:, :, :], bank[0][:, :].rearrange("p (t f) -> p t f", t=NT),
                              bc(rs[:, 3, :], 2, E), ALU.mult).then_inc(s["xn_ready"], 1)
            dve.wait_ge(s["x_psum"], 2)
            dve.tensor_copy(xT[:, 4:8, :], bank[3][:, 0:256].rearrange("p (a j) -> p a j", a=4))\
                .then_inc(s["xT_ready"], 1)
            dve.wait_ge(s["q_psum"], 1)
            dve.wait_ge(s["set_pool"], 10)
            dve.tensor_scalar(q_bd[64:128, :, 64:128], bank[4][64:128, :].rearrange("p (a j) -> p a j", a=NP),
                              E ** -0.5, None, ALU.mult).then_inc(s["q_ready"], 1)
            dve.wait_ge(s["kT_ready"], 1)
            for h in range(5):
                dve.tensor_scalar(k_h[:, h, :], kT[:, :], view(cst, CONST, "headmask")[:, h:h + 1], None,
                                  ALU.mult).then_inc(s["kh_ready"], 1)
            dve.wait_ge(s["cls_qkv"], 4)
            dve.wait_ge(s["v_psum"], 1)
            for i in range(2):
                for t in range(2):
                    src = bank[VB[t]][:, 0:256].rearrange("p (a b d) -> p a b d", a=NP, b=4)
                    r = slice(64 * i, 64 * i + 64)
                    dve.tensor_tensor(
                        vx[r, :, :, 2 * t + i, 0:D], src[r, :, :, :],
                        bc(vcls[r, :].rearrange("p (b h d) -> p b h d", b=4, h=2)[:, :, i, :], 1, NP),
                        ALU.subtract).then_inc(s["vx_ready"], 1)

            def class_query():
                dve.wait_ge(s["cq_psum"], 1)
                dve.tensor_copy(cq_cc[:, :], bank[2][:, 128:129]).then_inc(s["cq_cc_ready"], 1)
                dve.tensor_reduce(cq_m0[:, :], bank[1][:, :].rearrange("p (a j) -> p a j", a=NP), AX, ALU.max)\
                    .then_inc(s["cq_mx"], 1)
                dve.wait_ge(s["cq_mx"], 1)
                dve.wait_ge(s["cq_cc_ready"], 1)
                dve.tensor_scalar(cq_m[:, :], cq_m0[:, :], cq_cc[:, :], None, ALU.max).then_inc(s["cq_mx"], 1)
                dve.wait_ge(s["cq_mx"], 2)
                dve.tensor_tensor(cq_in[:, :, :], bank[1][:, :].rearrange("p (a j) -> p a j", a=NP),
                                  bc(cq_m[:, :], 2, J), ALU.subtract).then_inc(s["cq_in_ready"], 1)
                dve.tensor_tensor(cq_ci[:, :], cq_cc[:, :].broadcast_to([128, NP]), cq_m[:, :], ALU.subtract)\
                    .then_inc(s["cq_in_ready"], 1)

            def class_query_end():
                dve.wait_ge(s["cq_e_ready"], 2)
                dve.tensor_reduce(cq_s[:, :], cq_e[:, :, :], AX, ALU.add).then_inc(s["cq_s_ready"], 1)
                dve.wait_ge(s["vT_ready"], 1)
                dve.tensor_tensor(cq_v[:, :, :], cq_e[:, :, :], vT[:, :, :], ALU.mult).then_inc(s["cq_v_ready"], 1)
                dve.wait_ge(s["cq_s_ready"], 1)
                dve.scalar_tensor_tensor(cq_den[:, :], cq_c[:, :], 1.0 / 3.0, cq_s[:, :], ALU.mult, ALU.add)\
                    .then_inc(s["cq_den_ready"], 1)
                dve.wait_ge(s["cq_v_ready"], 1)
                dve.tensor_reduce(cq_n[:, :], cq_v[:, :, :], AX, ALU.add).then_inc(s["cq_n_ready"], 1)
                dve.wait_ge(s["cq_den_ready"], 1)
                dve.reciprocal(cq_r[:, :], cq_den[:, :]).then_inc(s["cq_r_ready"], 1)
                dve.wait_ge(s["cq_r_ready"], 1)
                dve.wait_ge(s["cq_n_ready"], 1)
                dve.tensor_tensor(cq_o[:, :], cq_n[:, :], cq_r[:, :], ALU.mult).then_inc(s["cq_o_ready"], 1)

            def softmax_in(p):
                sc = bank[3 + p % 2][:, :].rearrange("p (h k) -> p h k", h=H)
                dve.wait_ge(s["s_psum"], p + 1)
                dve.tensor_reduce(mx0[:, p, :], sc, AX, ALU.max).then_inc(s["mx0_ready"], 1)
                dve.wait_ge(s["mx0_ready"], p + 1)
                dve.tensor_tensor(mx[:, p, :], mx0[:, p, :], s_cls[:, p, :], ALU.max).then_inc(s["mx_ready"], 1)
                dve.wait_ge(s["mx_ready"], p + 1)
                if p >= 2:
                    dve.wait_ge(s["e_ready"], p - 1)
                dve.tensor_tensor(e_in[:, p % 2], sc, bc(mx[:, p, :], 2, J), ALU.subtract)\
                    .then_inc(s["ein_ready"], 1)

            def class_key(k):
                ps = slice(3 * k, min(3 * k + 3, NP))
                dve.tensor_tensor(ec_in[:, ps, :], s_cls[:, ps, :], mx[:, ps, :], ALU.subtract)\
                    .then_inc(s["ecin_ready"], 1)

            def normalise(k):
                ps = slice(3 * k, min(3 * k + 3, NP))
                n = ps.stop - ps.start
                pv = bank[k][:, 0:144 * n].rearrange("p (a t h c) -> p a t h c", a=4 * n, t=2, h=2)
                heads = lambda x, r=slice(0, 128): x[r, ps, :].rearrange("p a (b h) -> p (a b) h", h=2)
                dve.wait_ge(s["pv_psum"], ps.stop)
                dve.wait_ge(s["ec_ready"], k + 1)
                dve.scalar_tensor_tensor(heads(den), heads(ec), 1.0 / 3.0, pv[:, :, 0, :, D], ALU.mult, ALU.add)\
                    .then_inc(s["den_ready"], 1)
                dve.wait_ge(s["den_ready"], k + 1)
                dve.reciprocal(rden[:, ps, :], den[:, ps, :]).then_inc(s["rden_ready"], 1)
                dve.wait_ge(s["rden_ready"], k + 1)
                for t in range(2):
                    r = slice(64 * t, 64 * t + 64)
                    dve.tensor_tensor(o[r, ps].rearrange("p a b h d -> p (a b) h d"), pv[r, :, t, :, 0:D],
                                      bc(heads(rden, r), 3, D), ALU.mult).then_inc(s["o_ready"], 1)

            def table_factor():
                dve.wait_ge(s["rsum_psum"], 1)
                dve.wait_ge(s["in_toep"], 32)
                for t, n in ((0, 128), (1, J + 1)):
                    dve.scalar_tensor_tensor(cfac[0:n, t, :], bank[2][0:n, 8 * t:8 * t + 8], 1.0,
                                             tcls[0:n, t, :], ALU.add, ALU.add).then_inc(s["cfac_ready"], 1)

            class_query()
            dve.wait_ge(s["scls_ready"], 1)
            for p in range(NP):
                softmax_in(p)
                if p in (2, 5):
                    class_key(p // 3)
                if p == 2:
                    class_query_end()
                if p == 3:
                    table_factor()
                if p == 5:
                    normalise(0)
            class_key(2)
            normalise(1)
            normalise(2)

            dve.wait_ge(s["pvT_ready"], 1)
            dve.wait_ge(s["cq_o_ready"], 1)
            for g in range(G):
                dve.wait_ge(s["bT_psum"], g + 1)
                src = bank[g][:, 0:GC].rearrange("p (a q) -> p a q", a=2)
                for a in range(2):
                    dve.tensor_tensor(zz[:, g, a, 0:3 * J].rearrange("p (c j) -> p c j", c=3),
                                      src[:, a, 0:3 * J].rearrange("p (c j) -> p c j", c=3),
                                      bc(pvT[:, 2 * g + a, :], 1, 3), ALU.add).then_inc(s["zz_ready"], 1)
                dve.tensor_tensor(zz[:, g, :, S - 1], src[:, :, S - 1], cq_o[:, 2 * g:2 * g + 2], ALU.add)\
                    .then_inc(s["zz_ready"], 1)

            def scale(a, k, root_sem, r_sem):
                dve.wait_ge(s[root_sem], a + 1)
                dve.reciprocal(lr[0:CW, k, 2 * a:2 * a + 2, :], lroot[0:CW, k, 2 * a:2 * a + 2, :])\
                    .then_inc(s[r_sem], 1)

            for a in range(2):
                scale(a, 0, "lroot_ready", "lr_ready")
                for g in (2 * a, 2 * a + 1):
                    dve.wait_ge(s["lrb_psum"], g + 1)
                    dve.wait_ge(s["zg_ready"], g + 1)
                    dve.tensor_tensor(zr[:, g].rearrange("p a q -> p (a q)"), zg[:, g, :], bank[g][:, 0:GC],
                                      ALU.mult).then_inc(s["zr_ready"], 1)
                    dve.wait_ge(s["zr_ready"], g + 1)
                    dve.wait_ge(s["hb_ready"], 1)
                    for i in range(2):
                        dve.tensor_tensor(h2[:, g, i, 0:3 * J].rearrange("p (c j) -> p c j", c=3),
                                          zr[:, g, i, 0:3 * J].rearrange("p (c j) -> p c j", c=3),
                                          bc(hb[:, 2 * g + i, 0:J], 1, 3), ALU.add).then_inc(s["h2_ready"], 1)
                    dve.tensor_tensor(h2[:, g, :, S - 1], zr[:, g, :, S - 1], hb[:, 2 * g:2 * g + 2, J], ALU.add)\
                        .then_inc(s["h2_ready"], 1)
            for a in range(2):
                scale(a, 1, "hroot_ready", "hr_ready")
                for g in (2 * a, 2 * a + 1):
                    dve.wait_ge(s["hrb_psum"], g + 1)
                    dve.wait_ge(s["hc_ready"], g + 1)
                    dve.tensor_tensor(x2[:, g, :], hc[:, g, :], bank[g][:, 0:GC], ALU.mult)\
                        .then_inc(s["x2_ready"], 1)

            dve.wait_ge(s["w16_ready"], 3)
            for r in range(ROUNDS):
                src = w16[:, :] if r == 0 else cur[:, r % 2, :]
                dve.max(top8[:, r, :], src).then_inc(s["top_ready"], 1)
                dve.wait_ge(s["top_ready"], r + 1)
                if r < ROUNDS - 1:
                    dve.match_replace(cur[:, (r + 1) % 2, :], top8[:, r, :], src, -3.0e38)\
                        .then_inc(s["rep_ready"], 1)
                    dve.wait_ge(s["rep_ready"], r + 1)
            last = top8[:, ROUNDS - 1, (KEEP - 1) % 8:(KEEP - 1) % 8 + 1]
            dve.tensor_scalar(gt[:, :], w16[:, :], last, None, ALU.is_gt, ALU.add, accum_out=ngt[:, :])\
                .then_inc(s["gt_ready"], 1)
            dve.tensor_scalar(eq[:, :], w16[:, :], last, None, ALU.is_equal).then_inc(s["eq_ready"], 1)
            dve.wait_ge(s["gt_ready"], 1)
            dve.tensor_scalar(left[:, :], ngt[:, :], -1.0, float(KEEP), ALU.mult, ALU.add)\
                .then_inc(s["gt_ready"], 1)
            dve.wait_ge(s["eq_ready"], 1)
            dve.tensor_tensor_scan(cum[:, :], eq[:, :], zero16[:, :], 0.0, ALU.add, ALU.add)\
                .then_inc(s["cum_ready"], 1)
            dve.wait_ge(s["cum_ready"], 1)
            dve.wait_ge(s["gt_ready"], 2)
            dve.scalar_tensor_tensor(tie[:, :], cum[:, :], left[:, :], eq[:, :], ALU.is_le, ALU.mult)\
                .then_inc(s["chosen_ready"], 1)
            dve.wait_ge(s["chosen_ready"], 1)
            dve.tensor_tensor(chosen[:, :], tie[:, :], gt[:, :], ALU.add).then_inc(s["chosen_ready"], 1)
            dve.wait_ge(s["chosen_ready"], 2)
            dve.tensor_tensor(mw[:, 0:S - 1], chosen[:, 1:S], w16[:, 1:S], ALU.mult).then_inc(s["mw_ready"], 1)
            dve.tensor_tensor(mw[:, S - 1:S], chosen[:, 0:1], w16[:, 0:1], ALU.mult).then_inc(s["mw_ready"], 1)
            for g in range(G):
                dve.wait_ge(s["f2_psum"], 4 * g + 4)
                dve.wait_ge(s["mwb_ready"], g + 1)
                dve.scalar_tensor_tensor(yw[:, g, :], bank[YB[g]][:, 0:GC],
                                         view(tkw, TOKW, "ffn_b2"), mwb[:, g, :], ALU.add, ALU.mult)\
                    .then_inc(s["yw_ready"], 1)
                dve.wait_ge(s["yw_ready"], g + 1)
                dve.wait_ge(s["xh_ready"], g + 1)
                dve.tensor_tensor(res[:, g, :], yw[:, g, :], xh[:, g, :], ALU.add).then_inc(s["res_ready"], 1)

        @block.tensor
        def _(pe):
            pe.wait_ge(s["set_pool"], 3)
            pe.wait_ge(s["gw_ready"], 2)
            for c in range(2):
                last = pe.matmul(bank[0][0:PK, 0:E], inv_pf[:, :], gw[:, c, :], start=(c == 0), stop=(c == 1))
            last.then_inc(s["colmean_ready"], 1)
            for c in range(2):
                pe.matmul(bank[1][:, 0:E], w1p[:, 2 * E + 2 + c:2 * E + 3 + c].broadcast_to([PK, 128]),
                          w1[:, c, :], start=(c == 0), stop=(c == 1))
            pe.wait_ge(s["in_tokw"], 16)
            pe.matmul(bank[1][:, E:2 * E], view(tkw, TOKW, "b2")[0:64, :].broadcast_to([64, 128]),
                      view(tkw, TOKW, "wp1")[0:64, :], start=True, stop=True).then_inc(s["c_raw_ready"], 1)
            pe.wait_ge(s["gwf_ready"], 1)
            for t in range(NT):
                pe.wait_ge(s["in_fm0" if t < 4 else "in_fm1"], 16)
                for c in range(2):
                    last = pe.matmul(bank[2 + t // 4][:, 64 * (t % 4):64 * (t % 4) + 64],
                                     pfm[:, c, 128 * t:128 * t + 128], gwf[:, c, :],
                                     start=(c == 0), stop=(c == 1))
                if t % 4 == 3:
                    last.then_inc(s["y_proj"], 1)
            pe.wait_ge(s["in_const"], 16)
            for a in range(2):
                pe.wait_ge(s["y_ready"], a + 1)
                for i in range(2):
                    tq = 2 * a + i
                    last = pe.transpose(bank[4 + a][:, 128 * i:128 * i + 128],
                                        y[:, 2 * tq:2 * tq + 2, :].rearrange("p t f -> p (t f)"), ident)
                last.then_inc(s["yT_psum"], 1)
            pe.wait_ge(s["wg_bd_ready"], 2)
            for tq in range(4):
                pe.wait_ge(s["yT_ready"], tq // 2 + 1)
                last = pe.matmul(bank[6][:, 128 * tq:128 * tq + 128], yT[:, tq, :], wg_bd[:, :],
                                 start=True, stop=True)
            last.then_inc(s["z_psum"], 1)
            pe.wait_ge(s["xcls_ready"], 1)
            pe.matmul(bank[3][:, 0:1], xcls[0:1, :, :].rearrange("p a f -> p (a f)"), ident[0:1, 0:1], start=True, stop=True)
            pe.matmul(bank[3][:, 1:2], row[0:1, 3 * E:5 * E], ident[0:1, 0:1], start=True, stop=True)\
                .then_inc(s["xclsT_psum"], 1)
            pe.wait_ge(s["zn_ready"], 1)
            for tq in range(4):
                last = pe.transpose(bank[7][:, 128 * tq:128 * tq + 128],
                                    zn[:, 2 * tq:2 * tq + 2, :].rearrange("p t f -> p (t f)"), ident)
            last.then_inc(s["zn_psum"], 1)
            pe.matmul(bank[0][:, :], ones_row[:, :], bc(crc[0:1, 2, :], 1, NT), start=True, stop=True)
            pe.wait_ge(s["xclsT_ready"], 1)
            pe.wait_ge(s["in_attw"], 16)
            for i, w in enumerate(("wq_bd", "wk_bd", "wv_bd")):
                pe.matmul(bank[2][:, i:i + 1], view(atw, ATTW, w), xclsT[:, :], start=True, stop=True)
            pe.matmul(bank[2][:, 64:128], xclsT[0:64, :].broadcast_to([64, 128]),
                      view(atw, ATTW, "wv")[0:64, :], start=True, stop=True).then_inc(s["cls_psum"], 1)
            pe.wait_ge(s["h1_ready"], 1)
            pe.wait_ge(s["wp2c_ready"], 2)
            for tq in range(4):
                last = pe.matmul(bank[0][:, 128 * tq:128 * tq + 128], h1T[:, 128 * tq:128 * tq + 128],
                                 wp2c_bd[:, :], start=False, stop=True, skip_group_check=True)
            last.then_inc(s["h_psum"], 1)
            pe.matmul(bank[1][:, :], view(tkw, TOKW, "wp2_bd"), h1T[:, :], start=True, stop=True)\
                .then_inc(s["hf_psum"], 1)
            pe.wait_ge(s["xn_ready"], 1)
            pe.wait_ge(s["cls_qkv"], 4)
            pe.wait_ge(s["hbc_ready"], 1)
            for tq in range(4):
                last = pe.transpose(bank[2 + tq // 2][:, 128 * (tq % 2):128 * (tq % 2) + 128],
                                    xn[:, 2 * tq:2 * tq + 2, :].rearrange("p t f -> p (t f)"), ident)
                if tq % 2:
                    last.then_inc(s["x_psum"], 1)
            pe.wait_ge(s["xT_ready"], 2)
            xTf = xT[:, :, :].rearrange("p a j -> p (a j)")
            pe.matmul(bank[5][:, :], view(atw, ATTW, "wk_bd"), xTf, start=True, stop=True)\
                .then_inc(s["k_psum"], 1)
            pe.matmul(bank[4][:, :], view(atw, ATTW, "wq_bd"), xTf, start=True, stop=True)\
                .then_inc(s["q_psum"], 1)
            for b in range(B):
                r = slice(64 * (b % 2), 64 * (b % 2) + 64)
                for i in range(2):
                    heads_i = view(atw, ATTW, "wv")[r, :].rearrange("p (b h d) -> p b h d", b=4, h=2)[:, :, i, :]
                    p = b // 2
                    last = pe.matmul(bank[VB[b % 2]][64 * i:64 * i + 64, 32 * p:32 * p + 32], xT[r, p, :],
                                     heads_i, start=True, stop=True)
            last.then_inc(s["v_psum"], 1)
            pe.matmul(bank[7][:, :], view(atw, ATTW, "wv_bd"), xTf, start=True, stop=True)\
                .then_inc(s["vt_psum"], 1)
            pe.wait_ge(s["qm_ready"], 2)
            pe.wait_ge(s["kT_ready"], 1)
            pe.wait_ge(s["hb_ready"], 1)
            pe.matmul(bank[1][:, :], qcls_m[:, :], kT[:, :], start=True, stop=True)
            pe.matmul(bank[2][:, 128:129], qcls_m[:, :], kcls[:, :], start=True, stop=True)\
                .then_inc(s["cq_psum"], 1)
            pe.wait_ge(s["cq_cc_ready"], 1)
            pe.wait_ge(s["q_ready"], 2)
            for p in range(NP):
                last = pe.matmul(bank[2][:, 8 * p:8 * p + 8], q_bd[:, p, :], kcls_m[:, :], start=True, stop=True)
            last.then_inc(s["scls_psum"], 1)

            def scores(p):
                if p >= 2:
                    pe.wait_ge(s["ein_ready"], p - 1)
                pe.matmul(bank[3 + p % 2][:, :], q_bd[:, p, :], k_h[:, :, 64 * p:64 * p + 64],
                          start=True, stop=True).then_inc(s["s_psum"], 1)

            def turn(p):
                pe.wait_ge(s["e_ready"], p + 1)
                if p >= 2:
                    pe.wait_ge(s["eT_ready"], p - 1)
                for b in range(4):
                    last = pe.transpose(bank[6 + p % 2][:, 128 * b:128 * b + 128],
                                        e[:, p % 2, 128 * b:128 * b + 128], ident)
                last.then_inc(s["eT_psum"], 1)

            def weigh(p):
                pe.wait_ge(s["eT_ready"], p + 1)
                k = p // 3
                for b in range(4):
                    c = 144 * (p % 3) + 36 * b
                    last = pe.matmul(bank[k][:, c:c + 36], eT[:, p % 2, b, :],
                                     vx[:, p, b].rearrange("p a c -> p (a c)"), start=True, stop=True)
                last.then_inc(s["pv_psum"], 1)

            def table(t, g):
                n = 2 * t + g
                rows_t = 128 if t == 0 else J + 1
                if n >= 1:
                    pe.wait_ge(s["tb0_ready"], n)
                out_v = bank[5][0:rows_t, :].rearrange("q (a t b c) -> q a t b c", a=4, t=2, b=4)
                for b in range(4):
                    last = pe.matmul(out_v[:, :, :, b, :].rearrange("q a t c -> q (a t) c"),
                                     rT[:, b, 128 * t:128 * t + rows_t],
                                     vx[:, 4 * g:4 * g + 4, b, :, 0:D], start=True, stop=True)
                last.then_inc(s["tb_psum"], 1)

            def row_sums():
                for t, n in ((0, 128), (1, J + 1)):
                    for b in range(4):
                        last = pe.matmul(bank[2][0:n, 8 * t + 2 * b:8 * t + 2 * b + 2],
                                         rT[:, b, 128 * t:128 * t + n], half, start=True, stop=True)
                last.then_inc(s["rsum_psum"], 1)

            pe.wait_ge(s["kh_ready"], 8)
            scores(0)
            scores(1)
            pe.wait_ge(s["vx_ready"], 4)
            pe.wait_ge(s["set_pool"], 10)
            pe.wait_ge(s["vT_ready"], 1)
            for p in range(NP):
                turn(p)
                if p + 2 < NP:
                    scores(p + 2)
                if p == 0:
                    pe.wait_ge(s["cq_in_ready"], 2)
                    pe.wait_ge(s["scls_ready"], 1)
                if p == 1:
                    pe.wait_ge(s["rT_ready"], 2)
                if p in (1, 2, 4, 5):
                    table(*((0, 0), (0, 1), (1, 0), (1, 1))[(1, 2, 4, 5).index(p)])
                if p == 2:
                    row_sums()
                if p == 6:
                    pe.wait_ge(s["cfac_ready"], 2)
                weigh(p)
            pe.wait_ge(s["o_ready"], 6)
            pe.wait_ge(s["eT_ready"], NP)
            for p in range(NP):
                for t in range(2):
                    r = slice(64 * t, 64 * t + 64)
                    last = pe.matmul(bank[6][r, 64 * p:64 * p + 64], o[r, p].rearrange("p b h d -> p (b h d)"),
                                     ident[r, r], start=True, stop=True)
            last.then_inc(s["pvT_psum"], 1)
            pe.wait_ge(s["tb_ready"], 4)
            for g in range(G):
                for a in range(2):
                    b = 2 * (2 * g + a)
                    pe.transpose(bank[g][:, S * a:S * a + 128],
                                 tb[:, 0, b:b + 2, :].rearrange("p a f -> p (a f)"), ident)
                    last = pe.transpose(bank[g][:, S * a + 128:S * a + S],
                                        tb[0:J + 1, 1, b:b + 2, :].rearrange("p a f -> p (a f)"),
                                        ident[0:J + 1, 0:J + 1])
                last.then_inc(s["bT_psum"], 1)

            def centre(g, src):
                return pe.matmul(bank[4 + g][:, 0:GC], cent, src, start=True, stop=True)

            def variance(a, src):
                for i in range(2):
                    g = 2 * a + i
                    for c, (at, _) in enumerate(CH):
                        at = min(at, GC - CW)
                        last = pe.matmul(bank[2 * a][0:CW, 8 * i + 2 * c:8 * i + 2 * c + 2],
                                         src[:, g, at:at + CW], half, start=True, stop=True)
                return last

            def spread(a, k, out_sem):
                pe.wait_ge(s["in_pick"], 32)
                pe.transpose(bank[2 * a][0:16, 0:CW], lr[0:CW, k, 2 * a:2 * a + 2, :].rearrange("p g n -> p (g n)"),
                             ident[0:CW, 0:CW]).then_inc(s["lrt_psum"], 1)
                pe.wait_ge(s["lrT_ready"], 2 * k + a + 1)
                for i in range(2):
                    for c, (at, n) in enumerate(CH):
                        last = pe.matmul(bank[2 * a + i][:, at:at + n], sel16[:, 4 * i + c, :],
                                         lrT[:, k, a, 0:n], start=True, stop=True)
                    last.then_inc(s[out_sem], 1)

            pe.wait_ge(s["pvT_ready"], 1)
            for g in range(G):
                pe.wait_ge(s["zz_ready"], 3 * g + 3)
                centre(g, zz[:, g].rearrange("p a q -> p (a q)")).then_inc(s["zc_psum"], 1)
            for a in range(2):
                pe.wait_ge(s["zq_ready"], 2 * a + 2)
                variance(a, zq).then_inc(s["zvar_psum"], 1)
                pe.wait_ge(s["lr_ready"], a + 1)
                spread(a, 0, "lrb_psum")
            for a in range(2):
                for g in (2 * a, 2 * a + 1):
                    pe.wait_ge(s["h2_ready"], 3 * g + 3)
                    pe.wait_ge(s["zg_ready"], g + 1)
                    centre(g, h2[:, g].rearrange("p a q -> p (a q)")).then_inc(s["hc_psum"], 1)
            for a in range(2):
                pe.wait_ge(s["hq_ready"], 2 * a + 2)
                variance(a, hq).then_inc(s["hvar_psum"], 1)
                pe.wait_ge(s["hr_ready"], a + 1)
                spread(a, 1, "hrb_psum")

            def up(n):
                g, t, c = n // 4, (n // 2) % 2, n % 2
                pe.wait_ge(s["x2_ready"], g + 1 if n != 1 else 2)
                if n == 2:
                    pe.wait_ge(s["hc_ready"], 1)
                if n >= 3:
                    pe.wait_ge(s["gl_ready"], n - 2)
                r = slice(64 * t, 64 * t + 64)
                pe.matmul(bank[(0, 1, 4)[n % 3]][:, 0:GC],
                          view(ffw, FFNW, "ffn_w1")[r, 128 * c:128 * c + 128], x2[r, g, :],
                          start=True, stop=True).then_inc(s["f1_psum"], 1)

            def down(n):
                g, t, c = n // 4, (n // 2) % 2, n % 2
                pe.wait_ge(s["gl_ready"], n + 1)
                if n == 0:
                    pe.wait_ge(s["hc_ready"], 4)
                    pe.wait_ge(s["x2_ready"], 4)
                pe.matmul(bank[YB[g]][64 * t:64 * t + 64, 0:GC], view(ffw, FFNW, "ffn_w2")[:, 64 * c:64 * c + 64],
                          gl[:, n % 4, :], start=(c == 0), stop=(c == 1)).then_inc(s["f2_psum"], 1)

            pe.wait_ge(s["in_ffnw"], 16)
            up(0)
            up(1)
            pe.wait_ge(s["x2_ready"], 4)
            pe.wait_ge(s["hc_ready"], 4)
            wr = view(ffw, FFNW, "wr_bd")
            for t, n in ((0, 128), (1, J + 1)):
                for p in range(NP):
                    c = S * (p % 2) + 128 * t
                    last = pe.matmul(bank[6][0:n, B * t + 2 * p:B * t + 2 * p + 2], x2[:, p // 2, c:c + n], wr,
                                     start=True, stop=True)
            last.then_inc(s["w_psum"], 1)
            up(2)
            pe.wait_ge(s["wt_ready"], 2)
            pe.transpose(bank[6][0:B, 0:128], wt[:, 0, :], ident)
            pe.transpose(bank[6][0:B, 128:S], wt[0:J + 1, 1, :], ident[0:J + 1, 0:J + 1])\
                .then_inc(s["w16_psum"], 1)
            for n in range(3, 4 * G):
                up(n)
                down(n - 3)
            pe.wait_ge(s["mw_ready"], 2)
            pe.wait_ge(s["in_pick"], 32)
            for n in range(4 * G - 3, 4 * G):
                down(n)
            for g in range(G):
                if g == 1:
                    pe.wait_ge(s["gl_ready"], 4 * G)
                for a in range(2):
                    last = pe.matmul(bank[MB[g]][:, S * a:S * a + S], sel16[:, 2 * g + a, :], mw[:, :],
                                     start=True, stop=True)
                last.then_inc(s["mwb_psum"], 1)


def _lay_out(x, cls_tok, w):
    P = 8
    pt = x.reshape(4, 2, 2, 3, P, P, P, P)
    pt = pt.transpose(1, 4, 6, 0, 2, 5, 7, 3)
    ptm = np.ascontiguousarray(pt).reshape(128, NT, PF)
    pfm = np.ascontiguousarray(ptm.transpose(2, 1, 0).reshape(2, PK, NT * 128).transpose(1, 0, 2))
    col = lambda a: a.reshape(2, PK).T
    w1_pack = np.concatenate([w["L0_tok_W1"].reshape(2, PK, E).transpose(1, 0, 2).reshape(PK, 2 * E),
                              col(w["L0_tok_ln1_g"]), col(w["L0_tok_ln1_b"])], axis=1)
    twice = lambda a: np.concatenate([a.reshape(E, -1)] * 2, axis=0)

    def diag(a):
        out = np.zeros((128, 2 * a.shape[1]), np.float32)
        out[0:64, 0:a.shape[1]] = a
        out[64:128, a.shape[1]:] = a
        return out

    const = {"ident": np.eye(128), "cent": np.kron(np.eye(2), np.eye(64) - 1.0 / 64),
             "same_head": np.kron(np.eye(16), np.ones((8, 8))),
             "headmask": np.tile(np.kron(np.eye(8), np.ones((8, 1))), (2, 1)),
             "half": np.kron(np.eye(2), np.ones((64, 1)))}
    tokw = {"wp1": twice(w["L0_tok_Wp1"]), "wp2": twice(w["L0_tok_Wp2"]), "g2": twice(w["L0_tok_ln2_g"]),
            "b2": twice(w["L0_tok_ln2_b"]), "g3": twice(w["L0_tok_lnp_g"]), "b3": twice(w["L0_tok_lnp_b"]),
            "bp2": twice(w["L0_tok_bp2"]), "a_gamma": twice(w["L0_attn_ln_gamma"]),
            "a_beta": twice(w["L0_attn_ln_beta"]), "ffn_b2": twice(w["L0_ffn_b2"]),
            "wp2_bd": diag(w["L0_tok_Wp2"])}
    attw = {"wq_bd": diag(w["L0_attn_Wq"].T), "wk_bd": diag(w["L0_attn_Wk"].T),
            "wv_bd": diag(w["L0_attn_Wv"].T), "wv": twice(w["L0_attn_Wv"].T)}
    ffnw = {"ffn_w1": twice(w["L0_ffn_w1"]),
            "ffn_w2": w["L0_ffn_w2"].reshape(2, 128, E).transpose(1, 0, 2).reshape(128, 2 * E),
            "ffn_b1": w["L0_ffn_b1"].reshape(2, 128).T, "wr_bd": diag(w["L0_ffn_wr"])}
    pack = lambda fields, d: np.concatenate([d[n] for n, _ in fields], axis=1).astype(np.float32)
    rows = np.concatenate([w["L0_tok_b1"], w["L0_tok_bp1"], w["L0_tok_bp2"], cls_tok.reshape(-1),
                           cls_tok.reshape(-1)])
    table = w["L0_attn_bias_table"]
    at = np.arange(U)[None, :] + (J - 1) - np.arange(J)[:, None]
    toep = table[at].reshape(J, U, 4, 2).transpose(3, 0, 2, 1).reshape(128, 4, U)
    tc = np.zeros((2, 128, H), np.float32)
    tc[0] = table[S:S + 128]
    tc[1, 0:J] = table[S + 128:S + 3 * J]
    tc[1, J] = table[S - 1]
    pick = np.kron(np.eye(B), np.ones((1, 64))).reshape(B, NP, 128)
    return {"patches_tm": ptm, "patches_fm": pfm, "w1_pack": w1_pack, "const": pack(CONST, const),
            "rows": rows, "tokw": pack(TOKW, tokw), "attw": pack(ATTW, attw), "ffnw": pack(FFNW, ffnw),
            "toeplitz": toep, "table_cls": tc.transpose(1, 0, 2), "pick": pick.astype(np.float32),
            "br": w["L0_ffn_br"]}


def kernel(**inputs):
    import concourse.bacc as bacc
    from concourse.bass_utils import run_bass_kernel_spmd

    w = {k: np.asarray(v) for k, v in inputs.items()}
    arrays = {k: np.ascontiguousarray(v) for k, v in _lay_out(w["x"], w["cls_tok"], w).items()}
    nc = bacc.Bacc("TRN2", target_bir_lowering=False, num_devices=1)
    args = {k: nc.dram_tensor(k, a.shape, F32, kind="ExternalInput").ap() for k, a in arrays.items()}
    out = nc.dram_tensor("out", (128, G, GC), F32, kind="ExternalOutput").ap()
    build(nc, out=out, **args)
    got = run_bass_kernel_spmd(nc, [arrays], core_ids=[0]).results[0]["out"]
    got = got.reshape(2, E, NP, S).transpose(2, 0, 3, 1).reshape(B, S, E)
    return np.concatenate([got[:, S - 1:], got[:, :S - 1]], axis=1)
```

```python
from contextlib import ExitStack

import numpy as np
import concourse.bass as bass
from concourse import mybir

F32 = mybir.dt.float32
I32 = mybir.dt.int32
ALU = mybir.AluOpType
ACT = mybir.ActivationFunctionType
AX = mybir.AxisListType.X

B, J, E, H, D = 16, 64, 64, 8, 8
NP = B // 2
S = 3 * J + 1
PF = 192
PK = PF // 2
NT = 8
HID = 256
U = S + 2 * J
KEEP = int(0.5 * S) - 1
ROUNDS = (KEEP + 7) // 8
G = 4
GC = 2 * S
BT = (5, 3, 4, 2)
CB = (6, 7, 5, 3)
RB = (0, 1, 4, 2)
UB = (0, 1, 4)
MB = (2, 0, 1, 4)
KB, QB = (4, 6), (7, 5)
HB = (0, 5)
PVB = (0, 1, 2, 0)
TABLE = [(0, 0), (0, 1), (1, 0), (1, 1)]
TABLE_AT = (0, 2, 3, 4)
LN_EXP = "natural_log_exp_and_others"
EPS = 1e-5

CONST = [("ident", 128), ("cent", 128), ("same_head", 128), ("headmask", 8), ("half", 2), ("twice_ident", 64),
         ("same_image", 128)]
TOKW = [("wp1", 64), ("wp2", 64), ("g2", 1), ("b2", 1), ("g3", 1), ("b3", 1), ("bp2", 1),
        ("a_gamma", 1), ("a_beta", 1), ("ffn_b2", 1), ("wp2_bd", 128)]
ATTW = [("wq_bd", 128), ("wk_bd", 128), ("wv_bd", 128), ("wv", 64), ("wv_pair", 128)]
FFNW = [("ffn_w1", 256), ("ffn_w2", 128), ("ffn_b1", 2), ("wr_rows", NP * B)]


def columns(fields):
    at, out = 0, {}
    for name, n in fields:
        out[name] = (at, at + n)
        at += n
    return out, at


def bc(ap, axis, n):
    shape = list(ap.shape)
    return ap.unsqueeze(axis).broadcast_to(shape[:axis] + [n] + shape[axis:])


def build(nc, patches_tm, patches_fm, w1_pack, const, rows, tokw, attw, ffnw, toeplitz, table_cls,
          pick, br, out):
    with ExitStack() as ctx:
        def sb(name, *shape):
            return ctx.enter_context(nc.sbuf_tensor(name, list(shape), F32))

        def sem(name):
            return ctx.enter_context(nc.semaphore(name))

        bank = [ctx.enter_context(nc.psum_tensor(f"bank{i}", [128, 512], F32)) for i in range(8)]

        ptm = sb("ptm", 128, NT, PF)
        pfm = sb("pfm", PK, 2, NT * 128)
        w1p = sb("w1p", PK, 2 * E + 4)
        cst = sb("cst", 128, columns(CONST)[1])
        row = sb("row", 128, 5 * E)
        tkw = sb("tkw", 128, columns(TOKW)[1])
        atw = sb("atw", 128, columns(ATTW)[1])
        ffw = sb("ffw", 128, columns(FFNW)[1])
        toep = sb("toep", 128, 4, U)
        tcls = sb("tcls", 128, 2, H)
        sel16 = sb("sel16", B, NP, 128)
        br16 = sb("br16", B, 1)

        def view(tile, fields, name):
            a, b = columns(fields)[0][name]
            return tile[:, a:b]

        ident, cent = view(cst, CONST, "ident"), view(cst, CONST, "cent")
        half, same_image = view(cst, CONST, "half"), view(cst, CONST, "same_image")
        w1 = w1p[:, 0:2 * E].rearrange("p (c f) -> p c f", c=2)

        eps = sb("eps", 128, 1)
        inv_pf = sb("inv_pf", PK, PK)
        ones_row = sb("ones_row", 1, 128)
        gw = sb("gw", PK, 2, E)
        gwc = sb("gwc", PK, 2, E)
        gws = sb("gws", PK, 2)
        gwf = sb("gwf", PK, 2, E)
        cr = sb("cr", 128, 4, E)
        crs = sb("crs", 128, 4)
        crc = sb("crc", 128, 4, E)
        wg = sb("wg", 128, E)
        wgs = sb("wgs", 128, 1)
        wg_bd = sb("wg_bd", 128, 128)
        wp2s = sb("wp2s", 128, 1)
        wp2c_bd = sb("wp2c_bd", 128, 128)
        st = sb("st", 128, NT, 6)
        st_d = sb("st_d", 128, NT)
        st_s = sb("st_s", 128, NT)
        st_q = sb("st_q", 128, NT)
        st_v = sb("st_v", 128, NT)
        lnv = sb("lnv", 128, 5, NT)
        rs = sb("rs", 128, 5, NT)
        ys = sb("ys", 128, NT, E)
        y = sb("y", 128, NT, E)
        sq = sb("sq", 128, NT, E)
        ss = sb("ss", 128, 4, NT)
        yT = sb("yT", 128, 4, 128)
        zs = sb("zs", 128, NT, E)
        z = sb("z", 128, NT, E)
        zn = sb("zn", 128, NT, E)
        h1T = sb("h1T", 128, 512)
        hbias = sb("hbias", 128, 1)
        hb = sb("hb", 128, NP, J + 1)
        hs = sb("hs", 128, NT, E)
        xn = sb("xn", 128, NT, E)
        xT = sb("xT", 128, NP, J)
        xTm = sb("xTm", 128, NP, J)
        csq = sb("csq", 128, E)
        xcls = sb("xcls", 128, 2, E)
        xclsT = sb("xclsT", 128, 1)
        qcls = sb("qcls", 128, 1)
        kcls = sb("kcls", 128, 1)
        vcls = sb("vcls", 128, E)
        qcls_m = sb("qcls_m", 128, 128)
        kcls_m = sb("kcls_m", 128, H)
        kT = sb("kT", 128, NP * J)
        q_bd = sb("q_bd", 128, NP, 128)
        k_h = sb("k_h", 128, H, NP * J)
        vT = sb("vT", 128, NP, J)
        vx = sb("vx", 128, NP, 4, 4, 9)
        s_cls = sb("s_cls", 128, NP, H)
        mx0 = sb("mx0", 128, NP, H)
        mx = sb("mx", 128, NP, H)
        e_in = sb("e_in", 128, 2, H, J)
        e = sb("e", 128, 2, H * J)
        eT = sb("eT", 128, 2, 4, 128)
        ec_in = sb("ec_in", 128, NP, H)
        ec = sb("ec", 128, NP, H)
        den = sb("den", 128, NP, H)
        rden = sb("rden", 128, NP, H)
        o = sb("o", 128, NP, 2, 4, 2, D)
        pvT = sb("pvT", 128, NP, J)
        cq_cc = sb("cq_cc", 128, 1)
        cq_m0 = sb("cq_m0", 128, NP)
        cq_m = sb("cq_m", 128, NP)
        cq_in = sb("cq_in", 128, NP, J)
        cq_e = sb("cq_e", 128, NP, J)
        cq_ci = sb("cq_ci", 128, NP)
        cq_c = sb("cq_c", 128, NP)
        cq_s = sb("cq_s", 128, NP)
        cq_den = sb("cq_den", 128, NP)
        cq_r = sb("cq_r", 128, NP)
        cq_v = sb("cq_v", 128, NP, J)
        cq_n = sb("cq_n", 128, NP)
        cq_o = sb("cq_o", 128, NP)
        fold1 = sb("fold1", 128, 4, S)
        fold = sb("fold", 128, 4, S)
        rT = sb("rT", 128, 4, S)
        cfac0 = sb("cfac0", 128, 2, H)
        cfac = sb("cfac", 128, 2, H)
        cterm = sb("cterm", 128, 2, H, D)
        tb = sb("tb", 128, 2, B, E)
        zz = sb("zz", 128, G, 2, S)
        zq = sb("zq", 128, G, GC)
        rstd = sb("rstd", 128, G, GC)
        zr = sb("zr", 128, G, 2, S)
        h2 = sb("h2", 128, G, 2, S)
        x2 = sb("x2", 128, G, GC)
        xh = sb("xh", 128, G, GC)
        gl = k_h[:, :, :].rearrange("p h n -> p (h n)")[:, 0:4 * GC].rearrange("p (a n) -> p a n", a=4)
        w16 = sb("w16", B, S)
        cur = sb("cur", B, 2, S)
        top8 = sb("top8", B, ROUNDS, 8)
        gt = sb("gt", B, S)
        ngt = sb("ngt", B, 1)
        eq = sb("eq", B, S)
        cum = sb("cum", B, S)
        zero16 = sb("zero16", B, S)
        left = sb("left", B, 1)
        tie = sb("tie", B, S)
        chosen = sb("chosen", B, S)
        mw = sb("mw", B, S)
        yb = zz[:, :, :, :].rearrange("p g a q -> p g (a q)")
        yw = zr[:, :, :, :].rearrange("p g a q -> p g (a q)")
        res = zq

        names = """
            in_tm0 in_tm1 in_tokw in_attw in_toep in_ffnw in_pick res01_ready res23_ready out_done
            set_pool fold1_ready rT_ready xclsT_ready xT_ready xT1_ready xTm_ready kT_ready
            kh1_ready cfac_ready cls_qkv cterm_ready tb0_ready tb_ready x2_ready xh_ready yw_ready
            in_w1 in_fm0 in_rows in_fm1 in_const ln_done st_v_ready rs1 crc_ready csq_ready y_ready
            sq_y yT_psum yT_ready ss_y rs2 css_ready rs_c z_ready sq_z ss_z rs3 zn_psum h1_ready
            ss_h rs4 x_psum k_psum q_psum q_ready kh0_ready scls_psum scls_ready ein_ready eT_psum
            e_ready tb_psum pv_psum eT_ready ecin_ready ec_ready pvT_psum pvT_ready v_psum vx_ready
            hf_psum hbias_ready hb_ready vt_psum vT_ready cq_in_ready cq_e_ready zc_psum hc_psum
            zq_ready hq_ready zvar_psum hvar_psum zrs_ready hrs_ready f2_psum yb_ready f1_psum
            gl_ready gw_ready colmean_ready gwc_ready gwf_ready st_ready st_d_ready c_raw_ready
            cr_ready y_proj ys_ready wg_ready wp2s_ready wg_bd_ready wp2c_ready z_psum zs_ready
            xcls_ready zn_ready xclsT_psum hbc_ready cls_psum qm_ready h_psum hs_ready crs_ready cr2_ready sq_h xn_ready
            q2_ready cq_psum cq_cc_ready cq_mx cq_s_ready cq_v_ready cq_den_ready cq_n_ready
            cq_r_ready cq_o_ready s_psum mx0_ready mx_ready den_ready rden_ready o_ready rsum_psum
            vx2_ready bT_psum zz_ready zr_ready h2_ready w16_psum w16_ready top_ready rep_ready
            gt_ready eq_ready cum_ready chosen_ready mw_ready mwb_psum
        """.split()
        s = {n: sem(n) for n in names}

        block = ctx.enter_context(nc.Block())

        @block.sync
        def _(sp):
            sp.dma_start(w1p[:, :], w1_pack).then_inc(s["in_w1"], 16)
            sp.dma_start(ptm[:, 0:4, :], patches_tm[:, 0:4, :]).then_inc(s["in_tm0"], 16)
            sp.dma_start(ptm[:, 4:8, :], patches_tm[:, 4:8, :]).then_inc(s["in_tm1"], 16)
            sp.dma_start(tkw[:, :], tokw).then_inc(s["in_tokw"], 16)
            sp.dma_start(atw[:, :], attw).then_inc(s["in_attw"], 16)
            sp.dma_start(toep[:, :, :], toeplitz).then_inc(s["in_toep"], 16)
            sp.dma_start(tcls[:, :, :], table_cls).then_inc(s["in_toep"], 16)
            sp.dma_start(ffw[:, :], ffnw).then_inc(s["in_ffnw"], 16)
            sp.dma_start(sel16[:, :, :], pick).then_inc(s["in_pick"], 16)
            sp.dma_start(br16[:, :], br.unsqueeze(0).broadcast_to([B, 1])).then_inc(s["in_pick"], 16)
            for i, g in enumerate((0, 2, 1, 3)):
                sp.wait_ge(s["res01_ready" if g < 2 else "res23_ready"], i // 2 + 1)
                sp.dma_start(out[:, g, :], res[:, g, :]).then_inc(s["out_done"], 16)
            sp.wait_ge(s["out_done"], 16 * G)

        @block.gpsimd
        def _(pool):
            pool.memset(eps[:, :], EPS).then_inc(s["set_pool"], 1)
            pool.memset(inv_pf[:, :], 1.0 / PF).then_inc(s["set_pool"], 1)
            pool.memset(ones_row[:, :], 1.0).then_inc(s["set_pool"], 1)
            pool.memset(wg_bd[:, :], 0.0).then_inc(s["set_pool"], 1)
            pool.memset(wp2c_bd[:, :], 0.0).then_inc(s["set_pool"], 1)
            pool.memset(zero16[:, :], 0.0).then_inc(s["set_pool"], 1)
            pool.memset(q_bd[:, :, :], 0.0).then_inc(s["set_pool"], 1)
            pool.memset(vx[:, :, :, :, :], 0.0).then_inc(s["set_pool"], 1)
            pool.memset(o[:, :, :, :, :, :].rearrange("p a t b h d -> p (a t b h d)"), 0.0)\
                .then_inc(s["set_pool"], 1)
            pool.wait_ge(s["set_pool"], 9)
            for h in range(2):
                pool.memset(vx[64 * h:64 * h + 64, :, :, h::2, 8:9].rearrange("p a b c d -> p (a b) (c d)"),
                            1.0).then_inc(s["set_pool"], 1)
            pool.wait_ge(s["set_pool"], 11)
            pool.wait_ge(s["in_toep"], 32)
            pool.tensor_tensor(fold1[:, :, :], toep[:, :, 0:S], toep[:, :, J:J + S], ALU.add)\
                .then_inc(s["fold1_ready"], 1)
            pool.wait_ge(s["fold1_ready"], 1)
            pool.tensor_tensor(fold[:, :, :], fold1[:, :, :], toep[:, :, 2 * J:2 * J + S], ALU.add)\
                .then_inc(s["fold1_ready"], 1)
            pool.wait_ge(s["fold1_ready"], 2)
            pool.tensor_copy(rT[:, :, 0:S - 1], fold[:, :, 1:S]).then_inc(s["rT_ready"], 1)
            pool.tensor_copy(rT[:, :, S - 1:S], fold[:, :, 0:1]).then_inc(s["rT_ready"], 1)
            pool.wait_ge(s["xclsT_ready"], 1)
            for a in range(2):
                pool.wait_ge(s["xT_ready" if a == 0 else "xT1_ready"], 1)
                pool.tensor_scalar(xTm[:, 4 * a:4 * a + 4, :], xT[:, 4 * a:4 * a + 4, :], xclsT[:, 0:1], None,
                                   ALU.subtract).then_inc(s["xTm_ready"], 1)
            pool.wait_ge(s["kT_ready"], 2)
            for h in range(4):
                pool.tensor_scalar(k_h[:, h, 256:512], kT[:, 256:512], view(cst, CONST, "headmask")[:, h:h + 1],
                                   None, ALU.mult).then_inc(s["kh1_ready"], 1)
            pool.wait_ge(s["cfac_ready"], 2)
            pool.wait_ge(s["cls_qkv"], 3)
            for t, n in ((0, 128), (1, J + 1)):
                pool.tensor_tensor(cterm[0:n, t, :, :], vcls[0:n, :].rearrange("p (h d) -> p h d", h=H),
                                   bc(cfac[0:n, t, :], 2, D), ALU.mult).then_inc(s["cterm_ready"], 1)
            pool.wait_ge(s["cterm_ready"], 2)
            for t in range(2):
                rows_t = 128 if t == 0 else J + 1
                for g in range(2):
                    pool.wait_ge(s["tb0_ready"], 2 * t + g + 1)
                    pool.tensor_tensor(
                        tb[0:rows_t, t, 8 * g:8 * g + 8, :], tb[0:rows_t, t, 8 * g:8 * g + 8, :],
                        bc(cterm[0:rows_t, t].rearrange("p h d -> p (h d)"), 1, 8), ALU.add)\
                        .then_inc(s["tb_ready"], 1)
            pool.wait_ge(s["cq_e_ready"], 2)
            pool.wait_ge(s["vT_ready"], 1)
            pool.tensor_tensor(cq_v[:, :, :], cq_e[:, :, :], vT[:, :, :], ALU.mult).then_inc(s["cq_v_ready"], 1)
            for g in range(G):
                pool.wait_ge(s["x2_ready"], g + 1)
                pool.tensor_tensor(xh[:, g, :], x2[:, g, :], h2[:, g].rearrange("p a q -> p (a q)"),
                                   ALU.add).then_inc(s["xh_ready"], 1)
            pool.wait_ge(s["xh_ready"], 2)
            for g in range(2):
                pool.wait_ge(s["yw_ready"], g + 1)
                pool.tensor_tensor(res[:, g, :], yw[:, g, :], xh[:, g, :], ALU.add).then_inc(s["res01_ready"], 1)

        @block.scalar
        def _(act):
            act.dma_start(pfm[:, :, 0:512], patches_fm[:, :, 0:512]).then_inc(s["in_fm0"], 16)
            act.dma_start(row[:, :], rows.unsqueeze(0).broadcast_to([128, 5 * E])).then_inc(s["in_rows"], 16)
            act.dma_start(pfm[:, :, 512:1024], patches_fm[:, :, 512:1024]).then_inc(s["in_fm1"], 16)
            act.dma_start(cst[:, :], const).then_inc(s["in_const"], 16)
            act.preload_act_table_set(LN_EXP)
            lns = [0]

            def inverse_std(dst, mid, src, scale, done):
                act.activation(mid, src, ACT.Ln, bias=eps[:, :], scale=scale).then_inc(s["ln_done"], 1)
                lns[0] += 1
                act.wait_ge(s["ln_done"], lns[0])
                return act.activation(dst, mid, ACT.Exp, scale=-0.5).then_inc(s[done], 1)

            act.wait_ge(s["set_pool"], 1)
            act.wait_ge(s["st_v_ready"], 1)
            inverse_std(rs[:, 0, :], lnv[:, 0, :], st_v[:, :], 1.0 / PF, "rs1")
            act.wait_ge(s["in_rows"], 16)
            act.activation(cr[:, 2:4, :].rearrange("p a f -> p (a f)"), row[:, 2 * E:4 * E], ACT.Copy)\
                .then_inc(s["cr2_ready"], 1)
            for a in range(2):
                t = slice(4 * a, 4 * a + 4)
                act.wait_ge(s["y_ready"], a + 1)
                act.activation(sq[:, t, :], y[:, t, :], ACT.Square).then_inc(s["sq_y"], 1)
                act.wait_ge(s["yT_psum"], a + 1)
                act.activation(yT[:, 2 * a:2 * a + 2, :], bank[4 + a][:, 0:256].rearrange("p (a n) -> p a n", a=2),
                               ACT.Copy).then_inc(s["yT_ready"], 1)
            act.wait_ge(s["crc_ready"], 2)
            act.activation(csq[:, :], crc[:, 3, :], ACT.Square).then_inc(s["csq_ready"], 1)
            act.wait_ge(s["ss_y"], 2)
            inverse_std(rs[:, 1, :], lnv[:, 1, :], ss[:, 0, :], 1.0 / E, "rs2")
            act.wait_ge(s["css_ready"], 1)
            inverse_std(rs[:, 4, 0:1], lnv[:, 4, 0:1], ss[:, 3, 0:1], 1.0 / E, "rs_c")
            for a in range(2):
                t = slice(4 * a, 4 * a + 4)
                act.wait_ge(s["z_ready"], a + 1)
                act.activation(sq[:, t, :], z[:, t, :], ACT.Square).then_inc(s["sq_z"], 1)
                act.wait_ge(s["ss_z"], a + 1)
                inverse_std(rs[:, 2, t], lnv[:, 2, t], ss[:, 1, t], 1.0 / E, "rs3")
            act.preload_act_table(ACT.Silu)
            for a in range(2):
                act.wait_ge(s["zn_psum"], a + 1)
                act.activation(h1T[:, 256 * a:256 * a + 256], bank[7 - a][:, 0:256], ACT.Silu,
                               bias=view(tkw, TOKW, "b3"), scale=view(tkw, TOKW, "g3")).then_inc(s["h1_ready"], 1)
            act.preload_act_table_set(LN_EXP)
            for a in range(2):
                t = slice(4 * a, 4 * a + 4)
                act.wait_ge(s["ss_h"], a + 1)
                inverse_std(rs[:, 3, t], lnv[:, 3, t], ss[:, 2, t], 1.0 / E, "rs4")
            act.wait_ge(s["x_psum"], 1)
            act.activation(xT[:, 0:4, :], bank[2][:, 0:256].rearrange("p (a j) -> p a j", a=4), ACT.Copy)\
                .then_inc(s["xT_ready"], 1)
            act.wait_ge(s["set_pool"], 7)

            def keys_queries(a):
                act.wait_ge(s["k_psum"], a + 1)
                act.activation(kT[:, 256 * a:256 * a + 256], bank[KB[a]][:, 0:256], ACT.Copy)\
                    .then_inc(s["kT_ready"], 1)
                act.wait_ge(s["q_psum"], a + 1)
                act.activation(q_bd[0:64, 4 * a:4 * a + 4, 0:64],
                               bank[QB[a]][0:64, 0:256].rearrange("p (a j) -> p a j", a=4),
                               ACT.Copy, scale=E ** -0.5).then_inc(s["q_ready"], 1)

            def head_keys(a, heads):
                act.wait_ge(s["kT_ready"], a + 1)
                for h in heads:
                    act.activation(k_h[:, h, 256 * a:256 * a + 256], kT[:, 256 * a:256 * a + 256], ACT.Copy,
                                   scale=view(cst, CONST, "headmask")[:, h:h + 1])\
                        .then_inc(s["kh0_ready" if a == 0 else "kh1_ready"], 1)

            def class_scores_out(a):
                act.wait_ge(s["scls_psum"], a + 1)
                act.activation(s_cls[:, 4 * a:4 * a + 4, :],
                               bank[2][:, 32 * a:32 * a + 32].rearrange("p (a h) -> p a h", a=4), ACT.Copy)\
                    .then_inc(s["scls_ready"], 1)

            def exps(p):
                act.wait_ge(s["ein_ready"], p + 1)
                if p >= 2:
                    act.wait_ge(s["eT_psum"], p - 1)
                act.activation(e[:, p % 2, :], e_in[:, p % 2].rearrange("p h k -> p (h k)"), ACT.Exp)\
                    .then_inc(s["e_ready"], 1)

            def table_out(t, g):
                n = 2 * t + g
                rows_t = 128 if t == 0 else J + 1
                act.wait_ge(s["tb_psum"], n + 1)
                act.activation(tb[0:rows_t, t, 8 * g:8 * g + 8, :],
                               bank[5][0:rows_t, :].rearrange("p (a f) -> p a f", a=8), ACT.Copy)\
                    .then_inc(s["tb0_ready"], 1)

            def weights_out(p):
                act.wait_ge(s["eT_psum"], p + 1)
                if p >= 2:
                    act.wait_ge(s["pv_psum"], p - 1)
                act.activation(eT[:, p % 2].rearrange("p a n -> p (a n)"), bank[6 + p % 2][:, :], ACT.Copy)\
                    .then_inc(s["eT_ready"], 1)

            def class_key_exp(g):
                act.wait_ge(s["ecin_ready"], g + 1)
                act.activation(ec[:, 2 * g:2 * g + 2, :], ec_in[:, 2 * g:2 * g + 2, :], ACT.Exp)\
                    .then_inc(s["ec_ready"], 1)

            def softmax_part_out(g):
                act.wait_ge(s["pvT_psum"], g + 1)
                act.activation(pvT[:, 2 * g:2 * g + 2, :],
                               bank[1][:, 128 * g:128 * g + 128].rearrange("p (a j) -> p a j", a=2), ACT.Copy)\
                    .then_inc(s["pvT_ready"], 1)

            keys_queries(0)
            head_keys(0, (5, 6, 7))
            keys_queries(1)
            class_scores_out(0)
            exps(0)
            act.wait_ge(s["v_psum"], 1)
            act.wait_ge(s["set_pool"], 8)
            act.activation(vx[0:64, :, :, 0::2, 0:D].rearrange("p a b t d -> p (a b) t d"),
                           bank[0][0:64, :].rearrange("p (a t d) -> p a t d", t=2, d=D), ACT.Copy)\
                .then_inc(s["vx_ready"], 1)
            head_keys(1, (6, 7))
            exps(1)
            weights_out(0)
            class_scores_out(1)
            act.wait_ge(s["hf_psum"], 1)
            act.wait_ge(s["hbias_ready"], 1)
            act.activation(hb[:, :, 0:J], bank[1][:, :].rearrange("p (a j) -> p a j", a=NP), ACT.Identity,
                           bias=hbias[:, :]).then_inc(s["hb_ready"], 1)
            table_out(*TABLE[0])
            for p in range(2, NP):
                exps(p)
                weights_out(p - 1)
                if p - 1 in TABLE_AT:
                    table_out(*TABLE[TABLE_AT.index(p - 1)])
                if p == 2:
                    act.wait_ge(s["vt_psum"], 1)
                    act.activation(vT[:, :, :], bank[5][:, :].rearrange("p (a j) -> p a j", a=NP), ACT.Copy)\
                        .then_inc(s["vT_ready"], 1)
                if p == 4:
                    act.wait_ge(s["cq_in_ready"], 2)
                    act.activation(cq_e[:, :, :], cq_in[:, :, :], ACT.Exp).then_inc(s["cq_e_ready"], 1)
                    act.activation(cq_c[:, :], cq_ci[:, :], ACT.Exp).then_inc(s["cq_e_ready"], 1)
                if p in (3, 5, 7):
                    class_key_exp((p - 3) // 2)
            weights_out(NP - 1)
            softmax_part_out(0)
            class_key_exp(3)
            softmax_part_out(1)
            softmax_part_out(2)

            def squares(name, g):
                act.wait_ge(s["zc_psum" if name == "z" else "hc_psum"], g + 1)
                act.activation(zq[:, g, :], bank[CB[g]][:, 0:GC], ACT.Square)\
                    .then_inc(s["zq_ready" if name == "z" else "hq_ready"], 1)

            def inverse_stds(name, g):
                act.wait_ge(s["zvar_psum" if name == "z" else "hvar_psum"], g + 1)
                inverse_std(rstd[:, g, :], rstd[:, g, :], bank[RB[g]][:, 0:GC], 1.0 / E,
                            "zrs_ready" if name == "z" else "hrs_ready")

            squares("z", 0)
            softmax_part_out(3)
            squares("z", 1)
            inverse_stds("z", 0)
            squares("z", 2)
            inverse_stds("z", 1)
            squares("z", 3)
            inverse_stds("z", 2)
            inverse_stds("z", 3)
            squares("h", 0)
            squares("h", 1)
            inverse_stds("h", 0)
            squares("h", 2)
            inverse_stds("h", 1)
            squares("h", 3)
            inverse_stds("h", 2)
            inverse_stds("h", 3)
            act.preload_act_table(ACT.Gelu_apprx_tanh)
            b1 = view(ffw, FFNW, "ffn_b1")

            def ffn_out(g):
                act.wait_ge(s["f2_psum"], 4 * g + 4)
                act.activation(yb[:, g, :], bank[CB[g]][:, 0:GC], ACT.Identity, bias=view(tkw, TOKW, "ffn_b2"))\
                    .then_inc(s["yb_ready"], 1)

            for n in range(4 * G):
                act.wait_ge(s["f1_psum"], n + 1)
                if n >= 4:
                    act.wait_ge(s["f2_psum"], n - 3)
                act.activation(gl[:, n % 4, :], bank[UB[n % 3]][:, 0:GC], ACT.Gelu_apprx_tanh,
                               bias=b1[:, n % 2:n % 2 + 1]).then_inc(s["gl_ready"], 1)
                if n >= 7 and n % 4 == 3:
                    ffn_out(n // 4 - 1)
            ffn_out(G - 1)

        @block.vector
        def _(dve):
            dve.wait_ge(s["in_w1"], 16)
            for c in range(2):
                dve.tensor_scalar(gw[:, c, :], w1[:, c, :], w1p[:, 2 * E + c:2 * E + c + 1], None, ALU.mult)\
                    .then_inc(s["gw_ready"], 1)
            dve.wait_ge(s["colmean_ready"], 1)
            dve.tensor_tensor(gwc[:, :, :], gw[:, :, :], bc(bank[0][0:PK, 0:E], 1, 2), ALU.subtract)\
                .then_inc(s["gwc_ready"], 1)
            dve.wait_ge(s["gwc_ready"], 1)
            dve.tensor_reduce(gws[:, :], gwc[:, :, :], AX, ALU.add).then_inc(s["gwc_ready"], 1)
            dve.wait_ge(s["gwc_ready"], 2)
            dve.scalar_tensor_tensor(gwf[:, :, :], bc(gws[:, :], 2, E), -1.0 / E, gwc[:, :, :],
                                     ALU.mult, ALU.add).then_inc(s["gwf_ready"], 1)
            for t in range(NT):
                dve.wait_ge(s["in_tm0" if t < 4 else "in_tm1"], 16)
                dve.bn_stats(st[:, t, :], ptm[:, t, :]).then_inc(s["st_ready"], 1)
            dve.wait_ge(s["st_ready"], NT)
            dve.tensor_tensor(st_d[:, :], st[:, :, 1], st[:, :, 4], ALU.subtract).then_inc(s["st_d_ready"], 1)
            dve.tensor_tensor(st_s[:, :], st[:, :, 2], st[:, :, 5], ALU.add).then_inc(s["st_d_ready"], 1)
            dve.wait_ge(s["st_d_ready"], 2)
            dve.tensor_tensor(st_q[:, :], st_d[:, :], st_d[:, :], ALU.mult).then_inc(s["st_d_ready"], 1)
            dve.wait_ge(s["st_d_ready"], 3)
            dve.scalar_tensor_tensor(st_v[:, :], st_q[:, :], PF / 4.0, st_s[:, :], ALU.mult, ALU.add)\
                .then_inc(s["st_v_ready"], 1)
            dve.wait_ge(s["in_rows"], 16)
            dve.wait_ge(s["c_raw_ready"], 1)
            dve.tensor_tensor(cr[:, 0:2, :].rearrange("p a f -> p (a f)"), bank[1][:, 0:2 * E], row[:, 0:2 * E],
                              ALU.add).then_inc(s["cr_ready"], 1)

            def centre_rows(r, k):
                dve.tensor_reduce(crs[:, r], cr[:, r, :], AX, ALU.add).then_inc(s["crs_ready"], 1)
                dve.wait_ge(s["crs_ready"], k + 1)
                dve.scalar_tensor_tensor(crc[:, r, :], bc(crs[:, r], 2, E), -1.0 / E, cr[:, r, :],
                                         ALU.mult, ALU.add).then_inc(s["crc_ready"], 1)

            dve.wait_ge(s["cr_ready"], 1)
            centre_rows(slice(0, 2), 0)
            dve.wait_ge(s["rs1"], 1)
            dve.wait_ge(s["crc_ready"], 1)
            for a in range(2):
                t = slice(4 * a, 4 * a + 4)
                dve.wait_ge(s["y_proj"], a + 1)
                dve.tensor_tensor(ys[:, t, :], bank[2 + a][:, 0:256].rearrange("p (t f) -> p t f", t=4),
                                  bc(rs[:, 0, t], 2, E), ALU.mult).then_inc(s["ys_ready"], 1)
                dve.wait_ge(s["ys_ready"], a + 1)
                dve.tensor_tensor(y[:, t, :], ys[:, t, :], bc(crc[:, 0, :], 1, 4), ALU.add)\
                    .then_inc(s["y_ready"], 1)
            dve.wait_ge(s["cr2_ready"], 1)
            centre_rows(slice(2, 4), 1)
            dve.wait_ge(s["in_tokw"], 16)
            dve.tensor_scalar(wg[:, :], view(tkw, TOKW, "wp1"), view(tkw, TOKW, "g2"), None, ALU.mult)\
                .then_inc(s["wg_ready"], 1)
            dve.tensor_reduce(wp2s[:, :], view(tkw, TOKW, "wp2"), AX, ALU.add).then_inc(s["wp2s_ready"], 1)
            dve.wait_ge(s["wg_ready"], 1)
            dve.tensor_reduce(wgs[:, :], wg[:, :], AX, ALU.add).then_inc(s["wg_ready"], 1)
            dve.wait_ge(s["wg_ready"], 2)
            dve.wait_ge(s["set_pool"], 5)
            for i in range(2):
                r = slice(64 * i, 64 * i + 64)
                dve.scalar_tensor_tensor(wg_bd[r, r], wgs[r, :].broadcast_to([64, E]), -1.0 / E, wg[r, :],
                                         ALU.mult, ALU.add).then_inc(s["wg_bd_ready"], 1)
            for a in range(2):
                t = slice(4 * a, 4 * a + 4)
                dve.wait_ge(s["sq_y"], a + 1)
                dve.tensor_reduce(ss[:, 0, t], sq[:, t, :], AX, ALU.add).then_inc(s["ss_y"], 1)
            dve.wait_ge(s["wp2s_ready"], 1)
            for i in range(2):
                r = slice(64 * i, 64 * i + 64)
                dve.scalar_tensor_tensor(wp2c_bd[r, r], wp2s[r, :].broadcast_to([64, E]), -1.0 / E,
                                         view(tkw, TOKW, "wp2")[r, :], ALU.mult, ALU.add)\
                    .then_inc(s["wp2c_ready"], 1)
            dve.wait_ge(s["csq_ready"], 1)
            dve.tensor_reduce(ss[:, 3, 0:1], csq[:, :], AX, ALU.add).then_inc(s["css_ready"], 1)
            dve.tensor_tensor(hbias[:, :], view(tkw, TOKW, "bp2"), view(tkw, TOKW, "a_beta"), ALU.add)\
                .then_inc(s["hbias_ready"], 1)
            dve.wait_ge(s["rs2"], 1)
            for a in range(2):
                t = slice(4 * a, 4 * a + 4)
                dve.wait_ge(s["z_psum"], a + 1)
                dve.tensor_tensor(zs[:, t, :], bank[(6, 1)[a]][:, 0:256].rearrange("p (t f) -> p t f", t=4),
                                  bc(rs[:, 1, t], 2, E), ALU.mult).then_inc(s["zs_ready"], 1)
            for a in range(2):
                t = slice(4 * a, 4 * a + 4)
                dve.wait_ge(s["zs_ready"], a + 1)
                dve.tensor_tensor(z[:, t, :], zs[:, t, :], bc(crc[:, 1, :], 1, 4), ALU.add)\
                    .then_inc(s["z_ready"], 1)
            dve.wait_ge(s["rs_c"], 1)
            dve.tensor_scalar(xcls[:, :, :], bc(crc[:, 3, :], 1, 2), rs[:, 4, 0:1], None, ALU.mult)\
                .then_inc(s["xcls_ready"], 1)
            for a in range(2):
                t = slice(4 * a, 4 * a + 4)
                dve.wait_ge(s["sq_z"], a + 1)
                dve.tensor_reduce(ss[:, 1, t], sq[:, t, :], AX, ALU.add).then_inc(s["ss_z"], 1)
            for a in range(2):
                t = slice(4 * a, 4 * a + 4)
                dve.wait_ge(s["rs3"], a + 1)
                dve.wait_ge(s["z_ready"], a + 1)
                dve.tensor_tensor(zn[:, t, :], z[:, t, :], bc(rs[:, 2, t], 2, E), ALU.mult)\
                    .then_inc(s["zn_ready"], 1)
            dve.wait_ge(s["xclsT_psum"], 1)
            dve.tensor_copy(xclsT[:, :], bank[3][:, 0:1]).then_inc(s["xclsT_ready"], 1)
            dve.tensor_scalar(hb[:, :, J], bank[3][:, 1:2].broadcast_to([128, NP]),
                              view(tkw, TOKW, "a_beta"), None, ALU.add).then_inc(s["hbc_ready"], 1)
            dve.wait_ge(s["cls_psum"], 1)
            dve.tensor_scalar(qcls[:, :], bank[2][:, 0:1], E ** -0.5, None, ALU.mult).then_inc(s["cls_qkv"], 1)
            dve.tensor_copy(kcls[:, :], bank[2][:, 1:2]).then_inc(s["cls_qkv"], 1)
            dve.tensor_copy(vcls[:, :], bank[2][:, 64:128]).then_inc(s["cls_qkv"], 1)
            dve.wait_ge(s["cls_qkv"], 2)
            dve.tensor_scalar(qcls_m[:, :], view(cst, CONST, "same_head"), qcls[:, :], None, ALU.mult)\
                .then_inc(s["qm_ready"], 1)
            dve.tensor_scalar(kcls_m[:, :], view(cst, CONST, "headmask"), kcls[:, :], None, ALU.mult)\
                .then_inc(s["qm_ready"], 1)
            for a in range(2):
                t = slice(4 * a, 4 * a + 4)
                dve.wait_ge(s["h_psum"], a + 1)
                dve.tensor_copy(hs[:, t, :], bank[HB[a]][:, 0:256].rearrange("p (t f) -> p t f", t=4))\
                    .then_inc(s["hs_ready"], 1)
                dve.wait_ge(s["hs_ready"], a + 1)
                dve.tensor_tensor(sq[:, t, :], hs[:, t, :], hs[:, t, :], ALU.mult).then_inc(s["sq_h"], 1)
                dve.wait_ge(s["sq_h"], a + 1)
                dve.tensor_reduce(ss[:, 2, t], sq[:, t, :], AX, ALU.add).then_inc(s["ss_h"], 1)
            for a in range(2):
                t = slice(4 * a, 4 * a + 4)
                dve.wait_ge(s["rs4"], a + 1)
                dve.tensor_tensor(xn[:, t, :], hs[:, t, :], bc(rs[:, 3, t], 2, E), ALU.mult)\
                    .then_inc(s["xn_ready"], 1)
            dve.wait_ge(s["rsum_psum"], 1)
            dve.wait_ge(s["in_toep"], 32)
            for t, n in ((0, 128), (1, J + 1)):
                dve.scalar_tensor_tensor(cfac[0:n, t, :], bank[6][0:n, 8 * t:8 * t + 8], 1.0,
                                         tcls[0:n, t, :], ALU.add, ALU.add).then_inc(s["cfac_ready"], 1)
            dve.tensor_copy(cq_cc[:, :], bank[6][:, 16:17]).then_inc(s["cq_cc_ready"], 1)
            dve.wait_ge(s["x_psum"], 2)
            dve.tensor_copy(xT[:, 4:8, :], bank[3][:, 0:256].rearrange("p (a j) -> p a j", a=4))\
                .then_inc(s["xT1_ready"], 1)
            dve.wait_ge(s["set_pool"], 7)

            def queries(a):
                dve.wait_ge(s["q_psum"], a + 1)
                dve.tensor_scalar(q_bd[64:128, 4 * a:4 * a + 4, 64:128],
                                  bank[QB[a]][64:128, 0:256].rearrange("p (a j) -> p a j", a=4),
                                  E ** -0.5, None, ALU.mult).then_inc(s["q2_ready"], 1)

            def head_keys(a, heads):
                dve.wait_ge(s["kT_ready"], a + 1)
                for h in heads:
                    dve.tensor_scalar(k_h[:, h, 256 * a:256 * a + 256], kT[:, 256 * a:256 * a + 256],
                                      view(cst, CONST, "headmask")[:, h:h + 1], None, ALU.mult)\
                        .then_inc(s["kh0_ready" if a == 0 else "kh1_ready"], 1)

            def class_query():
                dve.wait_ge(s["cq_psum"], 1)
                dve.tensor_reduce(cq_m0[:, :], bank[2][:, :].rearrange("p (a j) -> p a j", a=NP), AX, ALU.max)\
                    .then_inc(s["cq_mx"], 1)
                dve.wait_ge(s["cq_mx"], 1)
                dve.wait_ge(s["cq_cc_ready"], 1)
                dve.tensor_scalar(cq_m[:, :], cq_m0[:, :], cq_cc[:, :], None, ALU.max).then_inc(s["cq_mx"], 1)
                dve.wait_ge(s["cq_mx"], 2)
                dve.tensor_tensor(cq_in[:, :, :], bank[2][:, :].rearrange("p (a j) -> p a j", a=NP),
                                  bc(cq_m[:, :], 2, J), ALU.subtract).then_inc(s["cq_in_ready"], 1)
                dve.tensor_tensor(cq_ci[:, :], cq_cc[:, :].broadcast_to([128, NP]), cq_m[:, :], ALU.subtract)\
                    .then_inc(s["cq_in_ready"], 1)

            def class_query_sums():
                dve.wait_ge(s["cq_e_ready"], 2)
                dve.tensor_reduce(cq_s[:, :], cq_e[:, :, :], AX, ALU.add).then_inc(s["cq_s_ready"], 1)
                dve.wait_ge(s["cq_s_ready"], 1)
                dve.scalar_tensor_tensor(cq_den[:, :], cq_c[:, :], 1.0 / 3.0, cq_s[:, :], ALU.mult, ALU.add)\
                    .then_inc(s["cq_den_ready"], 1)
                dve.wait_ge(s["cq_den_ready"], 1)
                dve.reciprocal(cq_r[:, :], cq_den[:, :]).then_inc(s["cq_r_ready"], 1)

            def class_query_end():
                dve.wait_ge(s["cq_v_ready"], 1)
                dve.tensor_reduce(cq_n[:, :], cq_v[:, :, :], AX, ALU.add).then_inc(s["cq_n_ready"], 1)
                dve.wait_ge(s["cq_r_ready"], 1)
                dve.wait_ge(s["cq_n_ready"], 1)
                dve.tensor_tensor(cq_o[:, :], cq_n[:, :], cq_r[:, :], ALU.mult).then_inc(s["cq_o_ready"], 1)

            def softmax_in(p):
                sc = bank[3 + p % 2][:, :].rearrange("p (h k) -> p h k", h=H)
                dve.wait_ge(s["s_psum"], p + 1)
                dve.tensor_reduce(mx0[:, p, :], sc, AX, ALU.max).then_inc(s["mx0_ready"], 1)
                dve.wait_ge(s["mx0_ready"], p + 1)
                dve.tensor_tensor(mx[:, p, :], mx0[:, p, :], s_cls[:, p, :], ALU.max).then_inc(s["mx_ready"], 1)
                dve.wait_ge(s["mx_ready"], p + 1)
                if p >= 2:
                    dve.wait_ge(s["e_ready"], p - 1)
                dve.tensor_tensor(e_in[:, p % 2], sc, bc(mx[:, p, :], 2, J), ALU.subtract)\
                    .then_inc(s["ein_ready"], 1)

            def class_key(g):
                ps = slice(2 * g, 2 * g + 2)
                dve.tensor_tensor(ec_in[:, ps, :], s_cls[:, ps, :], mx[:, ps, :], ALU.subtract)\
                    .then_inc(s["ecin_ready"], 1)

            def normalise(g):
                ps = slice(2 * g, 2 * g + 2)
                pv = bank[PVB[g]][:, 0:288].rearrange("p (a t h c) -> p a t h c", a=8, t=2, h=2)
                heads = lambda x, r=slice(0, 128): x[r, ps, :].rearrange("p a (b h) -> p (a b) h", h=2)
                dve.wait_ge(s["pv_psum"], ps.stop)
                dve.wait_ge(s["ec_ready"], g + 1)
                dve.scalar_tensor_tensor(heads(den), heads(ec), 1.0 / 3.0, pv[:, :, 0, :, D], ALU.mult, ALU.add)\
                    .then_inc(s["den_ready"], 1)
                dve.wait_ge(s["den_ready"], g + 1)
                dve.reciprocal(rden[:, ps, :], den[:, ps, :]).then_inc(s["rden_ready"], 1)
                dve.wait_ge(s["rden_ready"], g + 1)
                dve.wait_ge(s["set_pool"], 9)
                for t in range(2):
                    r = slice(64 * t, 64 * t + 64)
                    for a in range(2):
                        dve.tensor_tensor(o[r, 2 * g + a, t], pv[r, 4 * a:4 * a + 4, t, :, 0:D],
                                          bc(heads(rden, r)[:, 4 * a:4 * a + 4], 3, D), ALU.mult)\
                            .then_inc(s["o_ready"], 1)

            queries(0)
            head_keys(0, range(5))
            queries(1)
            dve.wait_ge(s["scls_ready"], 1)
            softmax_in(0)
            softmax_in(1)
            dve.wait_ge(s["v_psum"], 1)
            dve.wait_ge(s["set_pool"], 8)
            dve.tensor_copy(vx[64:128, :, :, 1::2, 0:D].rearrange("p a b t d -> p (a b) t d"),
                            bank[0][64:128, :].rearrange("p (a t d) -> p a t d", t=2, d=D))\
                .then_inc(s["vx2_ready"], 1)
            head_keys(1, (4, 5))
            class_key(0)
            for p in range(2, NP):
                if p == 4:
                    dve.wait_ge(s["scls_ready"], 2)
                softmax_in(p)
                if p % 2:
                    class_key(p // 2)
                if p == 3:
                    class_query()
                if p == 4:
                    normalise(0)
                if p == 5:
                    class_query_sums()
            normalise(1)
            class_query_end()
            normalise(2)

            def add_parts(g):
                dve.wait_ge(s["pvT_ready"], g + 1)
                dve.wait_ge(s["bT_psum"], g + 1)
                src = bank[BT[g]][:, 0:GC].rearrange("p (a q) -> p a q", a=2)
                for a in range(2):
                    dve.tensor_tensor(zz[:, g, a, 0:3 * J].rearrange("p (c j) -> p c j", c=3),
                                      src[:, a, 0:3 * J].rearrange("p (c j) -> p c j", c=3),
                                      bc(pvT[:, 2 * g + a, :], 1, 3), ALU.add).then_inc(s["zz_ready"], 1)
                dve.tensor_tensor(zz[:, g, :, S - 1], src[:, :, S - 1], cq_o[:, 2 * g:2 * g + 2], ALU.add)\
                    .then_inc(s["zz_ready"], 1)

            dve.wait_ge(s["cq_o_ready"], 1)
            add_parts(0)
            normalise(3)
            for g in range(1, G):
                add_parts(g)
            dve.wait_ge(s["hb_ready"], 1)
            dve.wait_ge(s["hbc_ready"], 1)
            def residual(g):
                dve.wait_ge(s["zrs_ready"], g + 1)
                dve.scalar_tensor_tensor(zr[:, g].rearrange("p a q -> p (a q)"), bank[CB[g]][:, 0:GC],
                                         view(tkw, TOKW, "a_gamma"), rstd[:, g, :], ALU.mult, ALU.mult)\
                    .then_inc(s["zr_ready"], 1)
                dve.wait_ge(s["zr_ready"], g + 1)
                for i in range(2):
                    dve.tensor_tensor(h2[:, g, i, 0:3 * J].rearrange("p (c j) -> p c j", c=3),
                                      zr[:, g, i, 0:3 * J].rearrange("p (c j) -> p c j", c=3),
                                      bc(hb[:, 2 * g + i, 0:J], 1, 3), ALU.add).then_inc(s["h2_ready"], 1)
                dve.tensor_tensor(h2[:, g, :, S - 1], zr[:, g, :, S - 1], hb[:, 2 * g:2 * g + 2, J], ALU.add)\
                    .then_inc(s["h2_ready"], 1)

            def norm(g):
                dve.wait_ge(s["hrs_ready"], g + 1)
                dve.tensor_tensor(x2[:, g, :], bank[CB[g]][:, 0:GC], rstd[:, g, :], ALU.mult)\
                    .then_inc(s["x2_ready"], 1)

            residual(0)
            residual(1)
            residual(2)
            residual(3)
            norm(0)
            norm(1)
            norm(2)
            norm(3)

            dve.wait_ge(s["w16_psum"], 1)
            dve.wait_ge(s["in_pick"], 32)
            dve.tensor_scalar(w16[:, 1:S], bank[2][0:B, 0:S - 1], br16[:, :], None, ALU.add)\
                .then_inc(s["w16_ready"], 1)
            dve.tensor_scalar(w16[:, 0:1], bank[2][0:B, S - 1:S], br16[:, :], None, ALU.add)\
                .then_inc(s["w16_ready"], 1)
            dve.wait_ge(s["w16_ready"], 2)
            for r in range(ROUNDS):
                src = w16[:, :] if r == 0 else cur[:, r % 2, :]
                dve.max(top8[:, r, :], src).then_inc(s["top_ready"], 1)
                dve.wait_ge(s["top_ready"], r + 1)
                if r < ROUNDS - 1:
                    dve.match_replace(cur[:, (r + 1) % 2, :], top8[:, r, :], src, -3.0e38)\
                        .then_inc(s["rep_ready"], 1)
                    dve.wait_ge(s["rep_ready"], r + 1)
            last = top8[:, ROUNDS - 1, (KEEP - 1) % 8:(KEEP - 1) % 8 + 1]
            dve.tensor_scalar(gt[:, :], w16[:, :], last, None, ALU.is_gt, ALU.add, accum_out=ngt[:, :])\
                .then_inc(s["gt_ready"], 1)
            dve.tensor_scalar(eq[:, :], w16[:, :], last, None, ALU.is_equal).then_inc(s["eq_ready"], 1)
            dve.wait_ge(s["gt_ready"], 1)
            dve.tensor_scalar(left[:, :], ngt[:, :], -1.0, float(KEEP), ALU.mult, ALU.add)\
                .then_inc(s["gt_ready"], 1)
            dve.wait_ge(s["eq_ready"], 1)
            dve.tensor_tensor_scan(cum[:, :], eq[:, :], zero16[:, :], 0.0, ALU.add, ALU.add)\
                .then_inc(s["cum_ready"], 1)
            dve.wait_ge(s["cum_ready"], 1)
            dve.wait_ge(s["gt_ready"], 2)
            dve.scalar_tensor_tensor(tie[:, :], cum[:, :], left[:, :], eq[:, :], ALU.is_le, ALU.mult)\
                .then_inc(s["chosen_ready"], 1)
            dve.wait_ge(s["chosen_ready"], 1)
            dve.tensor_tensor(chosen[:, :], tie[:, :], gt[:, :], ALU.add).then_inc(s["chosen_ready"], 1)
            dve.wait_ge(s["chosen_ready"], 2)
            dve.tensor_tensor(mw[:, 0:S - 1], chosen[:, 1:S], w16[:, 1:S], ALU.mult).then_inc(s["mw_ready"], 1)
            dve.tensor_tensor(mw[:, S - 1:S], chosen[:, 0:1], w16[:, 0:1], ALU.mult).then_inc(s["mw_ready"], 1)
            for g in range(G):
                dve.wait_ge(s["yb_ready"], g + 1)
                dve.wait_ge(s["mwb_psum"], g + 1)
                dve.tensor_tensor(yw[:, g, :], yb[:, g, :], bank[MB[g]][:, 0:GC], ALU.mult)\
                    .then_inc(s["yw_ready"], 1)
            dve.wait_ge(s["xh_ready"], G)
            for g in range(2, G):
                dve.wait_ge(s["yw_ready"], g + 1)
                dve.tensor_tensor(res[:, g, :], yw[:, g, :], xh[:, g, :], ALU.add).then_inc(s["res23_ready"], 1)

        @block.tensor
        def _(pe):
            pe.wait_ge(s["set_pool"], 1)

            def keep_busy(free, columns):
                for at in range(0, columns, 128):
                    pe.matmul(bank[free][:, 0:128], eps[:, :].broadcast_to([128, 128]),
                              eps[:, :].broadcast_to([128, 128]), start=True, stop=True)

            keep_busy(7, 768)
            pe.wait_ge(s["set_pool"], 3)
            pe.wait_ge(s["gw_ready"], 2)
            for c in range(2):
                last = pe.matmul(bank[0][0:PK, 0:E], inv_pf[:, :], gw[:, c, :], start=(c == 0), stop=(c == 1))
            last.then_inc(s["colmean_ready"], 1)
            keep_busy(7, 768)
            pe.wait_ge(s["gwf_ready"], 1)
            for t in range(NT):
                pe.wait_ge(s["in_fm0" if t < 4 else "in_fm1"], 16)
                for c in range(2):
                    last = pe.matmul(bank[2 + t // 4][:, 64 * (t % 4):64 * (t % 4) + 64],
                                     pfm[:, c, 128 * t:128 * t + 128], gwf[:, c, :],
                                     start=(c == 0), stop=(c == 1))
                if t % 4 == 3:
                    last.then_inc(s["y_proj"], 1)
                if t == 3:
                    for c in range(2):
                        pe.matmul(bank[1][:, 0:E], w1p[:, 2 * E + 2 + c:2 * E + 3 + c].broadcast_to([PK, 128]),
                                  w1[:, c, :], start=(c == 0), stop=(c == 1))
                    pe.wait_ge(s["in_tokw"], 16)
                    pe.matmul(bank[1][:, E:2 * E], view(tkw, TOKW, "b2")[0:64, :].broadcast_to([64, 128]),
                              view(tkw, TOKW, "wp1")[0:64, :], start=True, stop=True).then_inc(s["c_raw_ready"], 1)
            pe.wait_ge(s["in_const"], 16)
            for a in range(2):
                keep_busy(7, (256, 256)[a])
                pe.wait_ge(s["y_ready"], a + 1)
                for i in range(2):
                    tq = 2 * a + i
                    last = pe.transpose(bank[4 + a][:, 128 * i:128 * i + 128],
                                        y[:, 2 * tq:2 * tq + 2, :].rearrange("p t f -> p (t f)"), ident)
                last.then_inc(s["yT_psum"], 1)
            pe.wait_ge(s["wg_bd_ready"], 2)
            pe.wait_ge(s["cr_ready"], 1)
            for a in range(2):
                pe.wait_ge(s["yT_ready"], a + 1)
                for i in range(2):
                    last = pe.matmul(bank[(6, 1)[a]][:, 128 * i:128 * i + 128], yT[:, 2 * a + i, :], wg_bd[:, :],
                                     start=True, stop=True)
                last.then_inc(s["z_psum"], 1)
            keep_busy(2, 1024)
            pe.wait_ge(s["crc_ready"], 2)
            for a in range(2):
                pe.matmul(bank[HB[a]][:, 0:256], ones_row[:, :], bc(crc[0:1, 2, :], 1, 4), start=True, stop=True)
            pe.wait_ge(s["xcls_ready"], 1)
            pe.matmul(bank[3][:, 0:1], xcls[0:1, :, :].rearrange("p a f -> p (a f)"), ident[0:1, 0:1], start=True, stop=True)
            pe.matmul(bank[3][:, 1:2], row[0:1, 3 * E:5 * E], ident[0:1, 0:1], start=True, stop=True)\
                .then_inc(s["xclsT_psum"], 1)
            keep_busy(4, 256)
            for a in range(2):
                pe.wait_ge(s["zn_ready"], a + 1)
                for i in range(2):
                    tq = 2 * a + i
                    last = pe.transpose(bank[7 - a][:, 128 * i:128 * i + 128],
                                        zn[:, 2 * tq:2 * tq + 2, :].rearrange("p t f -> p (t f)"), ident)
                last.then_inc(s["zn_psum"], 1)
            pe.wait_ge(s["xclsT_ready"], 1)
            pe.wait_ge(s["in_attw"], 16)
            for i, w in enumerate(("wq_bd", "wk_bd")):
                pe.matmul(bank[2][:, i:i + 1], view(atw, ATTW, w), xclsT[:, :], start=True, stop=True)
            pe.matmul(bank[2][:, 64:128], xclsT[0:64, :].broadcast_to([64, 128]),
                      view(atw, ATTW, "wv")[0:64, :], start=True, stop=True).then_inc(s["cls_psum"], 1)
            pe.wait_ge(s["wp2c_ready"], 2)
            for a in range(2):
                pe.wait_ge(s["h1_ready"], a + 1)
                for i in range(2):
                    tq = 2 * a + i
                    last = pe.matmul(bank[HB[a]][:, 128 * i:128 * i + 128], h1T[:, 128 * tq:128 * tq + 128],
                                     wp2c_bd[:, :], start=False, stop=True, skip_group_check=True)
                last.then_inc(s["h_psum"], 1)
            pe.matmul(bank[1][:, :], view(tkw, TOKW, "wp2_bd"), h1T[:, :], start=True, stop=True)\
                .then_inc(s["hf_psum"], 1)
            pe.wait_ge(s["rT_ready"], 2)
            for t, n in ((0, 128), (1, J + 1)):
                for b in range(4):
                    pe.matmul(bank[6][0:n, 8 * t + 2 * b:8 * t + 2 * b + 2], rT[:, b, 128 * t:128 * t + n], half,
                              start=True, stop=True)
            pe.wait_ge(s["qm_ready"], 1)
            pe.matmul(bank[6][:, 16:17], qcls_m[:, :], kcls[:, :], start=True, stop=True)\
                .then_inc(s["rsum_psum"], 1)
            pe.wait_ge(s["cls_qkv"], 3)
            pe.wait_ge(s["hbc_ready"], 1)
            for a in range(2):
                pe.wait_ge(s["xn_ready"], a + 1)
                for i in range(2):
                    tq = 2 * a + i
                    last = pe.transpose(bank[2 + a][:, 128 * i:128 * i + 128],
                                        xn[:, 2 * tq:2 * tq + 2, :].rearrange("p t f -> p (t f)"), ident)
                last.then_inc(s["x_psum"], 1)
            for a in range(2):
                pe.wait_ge(s["xT_ready" if a == 0 else "xT1_ready"], 1)
                if a:
                    pe.wait_ge(s["cfac_ready"], 2)
                    pe.wait_ge(s["cq_cc_ready"], 1)
                xTa = xT[:, 4 * a:4 * a + 4, :].rearrange("p a j -> p (a j)")
                pe.matmul(bank[KB[a]][:, 0:256], view(atw, ATTW, "wk_bd"), xTa, start=True, stop=True)\
                    .then_inc(s["k_psum"], 1)
                pe.matmul(bank[QB[a]][:, 0:256], view(atw, ATTW, "wq_bd"), xTa, start=True, stop=True)\
                    .then_inc(s["q_psum"], 1)
            def class_scores(a):
                pe.wait_ge(s["qm_ready"], 2)
                pe.wait_ge(s["q_ready"], a + 1)
                pe.wait_ge(s["q2_ready"], a + 1)
                if a:
                    pe.wait_ge(s["scls_ready"], 1)
                for p in range(4 * a, 4 * a + 4):
                    last = pe.matmul(bank[2][:, 8 * p:8 * p + 8], q_bd[:, p, :], kcls_m[:, :],
                                     start=True, stop=True)
                last.then_inc(s["scls_psum"], 1)

            def values():
                pe.wait_ge(s["xTm_ready"], 2)
                for p in range(NP):
                    for i in range(2):
                        last = pe.matmul(bank[0][64 * i:64 * i + 64, 64 * p:64 * p + 64], xTm[:, p, :],
                                         view(atw, ATTW, "wv_pair")[:, 64 * i:64 * i + 64], start=True, stop=True)
                last.then_inc(s["v_psum"], 1)

            def class_query():
                pe.wait_ge(s["tb0_ready"], 1)
                pe.matmul(bank[5][:, :], view(atw, ATTW, "wv_bd"), xTm[:, :, :].rearrange("p a j -> p (a j)"),
                          start=True, stop=True).then_inc(s["vt_psum"], 1)
                pe.wait_ge(s["kT_ready"], 2)
                pe.wait_ge(s["scls_ready"], 2)
                pe.matmul(bank[2][:, :], qcls_m[:, :], kT[:, :], start=True, stop=True)\
                    .then_inc(s["cq_psum"], 1)

            def scores(p):
                if p >= 2:
                    pe.wait_ge(s["ein_ready"], p - 1)
                pe.matmul(bank[3 + p % 2][:, :], q_bd[:, p, :], k_h[:, :, 64 * p:64 * p + 64],
                          start=True, stop=True).then_inc(s["s_psum"], 1)

            def turn(p):
                pe.wait_ge(s["e_ready"], p + 1)
                if p >= 2:
                    pe.wait_ge(s["eT_ready"], p - 1)
                for b in range(4):
                    last = pe.transpose(bank[6 + p % 2][:, 128 * b:128 * b + 128],
                                        e[:, p % 2, 128 * b:128 * b + 128], ident)
                last.then_inc(s["eT_psum"], 1)

            def weigh(p):
                pe.wait_ge(s["eT_ready"], p + 1)
                k = PVB[p // 2]
                for b in range(4):
                    c = 144 * (p % 2) + 36 * b
                    last = pe.matmul(bank[k][:, c:c + 36], eT[:, p % 2, b, :],
                                     vx[:, p, b].rearrange("p a c -> p (a c)"), start=True, stop=True)
                last.then_inc(s["pv_psum"], 1)

            def table(t, g):
                n = 2 * t + g
                rows_t = 128 if t == 0 else J + 1
                if n >= 1:
                    pe.wait_ge(s["tb0_ready"], n)
                out_v = bank[5][0:rows_t, :].rearrange("q (a t b c) -> q a t b c", a=4, t=2, b=4)
                for b in range(4):
                    last = pe.matmul(out_v[:, :, :, b, :].rearrange("q a t c -> q (a t) c"),
                                     rT[:, b, 128 * t:128 * t + rows_t],
                                     vx[:, 4 * g:4 * g + 4, b, :, 0:D], start=True, stop=True)
                last.then_inc(s["tb_psum"], 1)

            def table_turn(g):
                if g == 0:
                    pe.wait_ge(s["tb_ready"], 4)
                for a in range(2):
                    b = 2 * (2 * g + a)
                    pe.transpose(bank[BT[g]][:, S * a:S * a + 128],
                                 tb[:, 0, b:b + 2, :].rearrange("p a f -> p (a f)"), ident)
                    last = pe.transpose(bank[BT[g]][:, S * a + 128:S * a + S],
                                        tb[0:J + 1, 1, b:b + 2, :].rearrange("p a f -> p (a f)"),
                                        ident[0:J + 1, 0:J + 1])
                last.then_inc(s["bT_psum"], 1)

            def softmax_turn(g):
                pe.wait_ge(s["o_ready"], 4 * g + 4)
                if g == 0:
                    pe.wait_ge(s["o_ready"], 8)
                else:
                    pe.wait_ge(s["pvT_ready"], g)
                for p in (2 * g, 2 * g + 1):
                    last = pe.matmul(bank[1][:, 64 * p:64 * p + 64], o[:, p].rearrange("p t b h d -> p (t b h d)"),
                                     view(cst, CONST, "twice_ident"), start=True, stop=True)
                last.then_inc(s["pvT_psum"], 1)

            pe.wait_ge(s["q_ready"], 1)
            pe.wait_ge(s["q2_ready"], 1)
            class_scores(0)
            keep_busy(3, 384)
            pe.wait_ge(s["kh0_ready"], 8)
            scores(0)
            scores(1)
            values()
            pe.wait_ge(s["vx_ready"], 1)
            pe.wait_ge(s["vx2_ready"], 1)
            pe.wait_ge(s["set_pool"], 11)
            for p in range(NP):
                turn(p)
                if p + 2 == 4:
                    pe.wait_ge(s["kh1_ready"], 8)
                if p + 2 < NP:
                    scores(p + 2)
                if p == 0:
                    class_scores(1)
                if p == 1:
                    class_query()
                if p == 2:
                    pe.wait_ge(s["vT_ready"], 1)
                if p in TABLE_AT:
                    table(*TABLE[TABLE_AT.index(p)])
                if p == 2:
                    pe.wait_ge(s["hb_ready"], 1)
                if p == 4:
                    pe.wait_ge(s["cq_in_ready"], 2)
                if p == 6:
                    pe.wait_ge(s["o_ready"], 4)
                    table_turn(0)
                if p == 7:
                    table_turn(1)
                if p >= 6:
                    keep_busy(p - 3, (256, 128)[p - 6])
                weigh(p)
            softmax_turn(0)
            table_turn(2)
            softmax_turn(1)
            pe.wait_ge(s["o_ready"], 12)
            table_turn(3)
            softmax_turn(2)

            def centre(name, g):
                if name == "z":
                    pe.wait_ge(s["zz_ready"], 3 * g + 3)
                    src = zz[:, g].rearrange("p a q -> p (a q)")
                else:
                    pe.wait_ge(s["h2_ready"], 3 * g + 3)
                    src = h2[:, g].rearrange("p a q -> p (a q)")
                pe.matmul(bank[CB[g]][:, 0:GC], cent, src, start=True, stop=True)\
                    .then_inc(s["zc_psum" if name == "z" else "hc_psum"], 1)

            def variance(name, g):
                pe.wait_ge(s["zq_ready" if name == "z" else "hq_ready"], g + 1)
                pe.matmul(bank[RB[g]][:, 0:GC], same_image, zq[:, g, :], start=True, stop=True)\
                    .then_inc(s["zvar_psum" if name == "z" else "hvar_psum"], 1)

            centre("z", 0)
            softmax_turn(3)
            centre("z", 1)
            variance("z", 0)
            pe.wait_ge(s["pvT_ready"], 4)
            centre("z", 2)
            variance("z", 1)
            centre("z", 3)
            variance("z", 2)
            variance("z", 3)
            centre("h", 0)
            centre("h", 1)
            variance("h", 0)
            centre("h", 2)
            variance("h", 1)
            centre("h", 3)
            variance("h", 2)
            variance("h", 3)

            def up(n):
                g, t, c = n // 4, (n // 2) % 2, n % 2
                pe.wait_ge(s["x2_ready"], g + 1)
                if n < 3:
                    pe.wait_ge(s["hrs_ready"], n + 1)
                else:
                    pe.wait_ge(s["gl_ready"], n - 2)
                r = slice(64 * t, 64 * t + 64)
                pe.matmul(bank[UB[n % 3]][:, 0:GC],
                          view(ffw, FFNW, "ffn_w1")[r, 128 * c:128 * c + 128], x2[r, g, :],
                          start=True, stop=True).then_inc(s["f1_psum"], 1)

            def down(n):
                g, t, c = n // 4, (n // 2) % 2, n % 2
                pe.wait_ge(s["gl_ready"], n + 1)
                pe.matmul(bank[CB[g]][64 * t:64 * t + 64, 0:GC], view(ffw, FFNW, "ffn_w2")[:, 64 * c:64 * c + 64],
                          gl[:, n % 4, :], start=(c == 0), stop=(c == 1)).then_inc(s["f2_psum"], 1)

            def route(pairs):
                for p in pairs:
                    pe.wait_ge(s["x2_ready"], p // 2 + 1)
                    last = pe.matmul(bank[2][0:B, 0:S], view(ffw, FFNW, "wr_rows")[:, B * p:B * p + B],
                                     x2[:, p // 2, S * (p % 2):S * (p % 2) + S],
                                     start=(p == 0), stop=(p == NP - 1))
                return last

            pe.wait_ge(s["in_ffnw"], 16)
            up(0)
            up(1)
            up(2)
            pe.wait_ge(s["hrs_ready"], 4)
            route(range(NP)).then_inc(s["w16_psum"], 1)
            for n in range(3, 4 * G):
                up(n)
                down(n - 3)
            for n in range(4 * G - 3, 4 * G):
                down(n)
            pe.wait_ge(s["mw_ready"], 2)
            pe.wait_ge(s["in_pick"], 32)
            for g in range(G):
                if g == 1:
                    pe.wait_ge(s["gl_ready"], 4 * G)
                for a in range(2):
                    last = pe.matmul(bank[MB[g]][:, S * a:S * a + S], sel16[:, 2 * g + a, :], mw[:, :],
                                     start=True, stop=True)
                last.then_inc(s["mwb_psum"], 1)


def _lay_out(x, cls_tok, w):
    P = 8
    pt = x.reshape(4, 2, 2, 3, P, P, P, P)
    pt = pt.transpose(1, 4, 6, 0, 2, 5, 7, 3)
    ptm = np.ascontiguousarray(pt).reshape(128, NT, PF)
    pfm = np.ascontiguousarray(ptm.transpose(2, 1, 0).reshape(2, PK, NT * 128).transpose(1, 0, 2))
    col = lambda a: a.reshape(2, PK).T
    w1_pack = np.concatenate([w["L0_tok_W1"].reshape(2, PK, E).transpose(1, 0, 2).reshape(PK, 2 * E),
                              col(w["L0_tok_ln1_g"]), col(w["L0_tok_ln1_b"])], axis=1)
    twice = lambda a: np.concatenate([a.reshape(E, -1)] * 2, axis=0)

    def diag(a):
        out = np.zeros((128, 2 * a.shape[1]), np.float32)
        out[0:64, 0:a.shape[1]] = a
        out[64:128, a.shape[1]:] = a
        return out

    const = {"ident": np.eye(128), "cent": np.kron(np.eye(2), np.eye(64) - 1.0 / 64),
             "same_head": np.kron(np.eye(16), np.ones((8, 8))),
             "headmask": np.tile(np.kron(np.eye(8), np.ones((8, 1))), (2, 1)),
             "half": np.kron(np.eye(2), np.ones((64, 1))), "twice_ident": np.tile(np.eye(64), (2, 1)),
             "same_image": np.kron(np.eye(2), np.ones((64, 64)))}
    tokw = {"wp1": twice(w["L0_tok_Wp1"]), "wp2": twice(w["L0_tok_Wp2"]), "g2": twice(w["L0_tok_ln2_g"]),
            "b2": twice(w["L0_tok_ln2_b"]), "g3": twice(w["L0_tok_lnp_g"]), "b3": twice(w["L0_tok_lnp_b"]),
            "bp2": twice(w["L0_tok_bp2"]), "a_gamma": twice(w["L0_attn_ln_gamma"]),
            "a_beta": twice(w["L0_attn_ln_beta"]), "ffn_b2": twice(w["L0_ffn_b2"]),
            "wp2_bd": diag(w["L0_tok_Wp2"])}
    wv_pair = np.zeros((2, E, 2, 4, 2, D), np.float32)
    for t in range(2):
        wv_pair[t, :, :, :, t, :] = w["L0_attn_Wv"].T.reshape(E, 4, 2, D).transpose(0, 2, 1, 3)
    wv_pair = wv_pair.reshape(128, 128)
    wr_rows = np.zeros((2, E, NP, B), np.float32)
    for b in range(B):
        wr_rows[b % 2, :, b // 2, b] = w["L0_ffn_wr"][:, 0]
    wr_rows = wr_rows.reshape(128, NP * B)
    attw = {"wq_bd": diag(w["L0_attn_Wq"].T), "wk_bd": diag(w["L0_attn_Wk"].T),
            "wv_bd": diag(w["L0_attn_Wv"].T), "wv": twice(w["L0_attn_Wv"].T), "wv_pair": wv_pair}
    ffnw = {"ffn_w1": twice(w["L0_ffn_w1"]),
            "ffn_w2": w["L0_ffn_w2"].reshape(2, 128, E).transpose(1, 0, 2).reshape(128, 2 * E),
            "ffn_b1": w["L0_ffn_b1"].reshape(2, 128).T, "wr_rows": wr_rows}
    pack = lambda fields, d: np.concatenate([d[n] for n, _ in fields], axis=1).astype(np.float32)
    rows = np.concatenate([w["L0_tok_b1"], w["L0_tok_bp1"], w["L0_tok_bp2"], cls_tok.reshape(-1),
                           cls_tok.reshape(-1)])
    table = w["L0_attn_bias_table"]
    at = np.arange(U)[None, :] + (J - 1) - np.arange(J)[:, None]
    toep = table[at].reshape(J, U, 4, 2).transpose(3, 0, 2, 1).reshape(128, 4, U)
    tc = np.zeros((2, 128, H), np.float32)
    tc[0] = table[S:S + 128]
    tc[1, 0:J] = table[S + 128:S + 3 * J]
    tc[1, J] = table[S - 1]
    pick = np.kron(np.eye(B), np.ones((1, 64))).reshape(B, NP, 128)
    return {"patches_tm": ptm, "patches_fm": pfm, "w1_pack": w1_pack, "const": pack(CONST, const),
            "rows": rows, "tokw": pack(TOKW, tokw), "attw": pack(ATTW, attw), "ffnw": pack(FFNW, ffnw),
            "toeplitz": toep, "table_cls": tc.transpose(1, 0, 2), "pick": pick.astype(np.float32),
            "br": w["L0_ffn_br"]}


def kernel(**inputs):
    import concourse.bacc as bacc
    from concourse.bass_utils import run_bass_kernel_spmd

    w = {k: np.asarray(v) for k, v in inputs.items()}
    arrays = {k: np.ascontiguousarray(v) for k, v in _lay_out(w["x"], w["cls_tok"], w).items()}
    nc = bacc.Bacc("TRN2", target_bir_lowering=False, num_devices=1)
    args = {k: nc.dram_tensor(k, a.shape, F32, kind="ExternalInput").ap() for k, a in arrays.items()}
    out = nc.dram_tensor("out", (128, G, GC), F32, kind="ExternalOutput").ap()
    build(nc, out=out, **args)
    got = run_bass_kernel_spmd(nc, [arrays], core_ids=[0]).results[0]["out"]
    got = got.reshape(2, E, NP, S).transpose(2, 0, 3, 1).reshape(B, S, E)
    return np.concatenate([got[:, S - 1:], got[:, :S - 1]], axis=1)
```
